# Optimizing a Trainium2 kernel written in Bass

```python
import numpy as np
import jax
import jax.numpy as jnp

def _softmax(x, axis=-1):
    return jax.nn.softmax(x, axis=axis)

def _gelu(x):
    return jax.nn.gelu(x, approximate=True)

def _silu(x):
    return jax.nn.silu(x)

def _sigmoid(x):
    return jax.nn.sigmoid(x)

def _layernorm(x, axis=-1, eps=1e-05):
    m = jnp.mean(x, axis=axis, keepdims=True)
    v = jnp.var(x, axis=axis, keepdims=True)
    return (x - m) / jnp.sqrt(v + eps)

def _scatter_add(tgt, idx, src, axis=0):
    return tgt.at[idx].add(src)

def _segment_sum(src, seg, n):
    return jax.ops.segment_sum(src, seg, n)
kernel_name = 'mk_cond_resid_d2_seqx_r8_15dd5c'

def setup_inputs(seed: int=0):
    np.random.seed(seed)
    _w = jnp.asarray

    def _rec_inputs():
        import jax
        import jax.numpy as jnp
        _rk = jax.random.key(seed)
        x = -0.000125 + 0.9999 * jax.random.normal(jax.random.fold_in(_rk, 1), (128, 32, 512), jnp.float32)
        _lenS = 32 - jax.random.randint(jax.random.fold_in(_rk, 7), (128,), 0, max(1, 32 // 4) + 1, jnp.int32)
        _lenS2 = 32 - jax.random.randint(jax.random.fold_in(_rk, 8), (128,), 0, max(1, 32 // 4) + 1, jnp.int32)
        itok_B_0_2 = jax.random.randint(jax.random.fold_in(_rk, 11), (128,), 0, 3, jnp.int32)
        itok_B_78_3631 = jax.random.randint(jax.random.fold_in(_rk, 12), (128,), 78, 454, jnp.int32)
        return (x, itok_B_0_2, itok_B_78_3631)
    x, itok_B_0_2, itok_B_78_3631 = _rec_inputs()

    def _L0_cond_setup():
        import jax, jax.numpy as jnp
        import numpy as np
        B, S, D_IN, D_OUT = (4, 256, 512, 512)
        R, NUM_LABELERS = (32, 5)
        LORA_SCALING = 16 / 32
        key = jax.random.key(seed)
        k1, k2, k3, k4, k5 = jax.random.split(key, 5)
        x = jax.random.normal(k1, (B, S, D_IN), dtype=jnp.float32)
        labeler_index = jax.random.randint(k2, (B,), 0, NUM_LABELERS, dtype=jnp.int64)
        W = jax.random.normal(k3, (D_OUT, D_IN), dtype=jnp.float32) * 0.02
        lora_A = jax.random.normal(k4, (NUM_LABELERS, D_IN, R), dtype=jnp.float32) * 0.02
        lora_B_w = jax.random.normal(k5, (D_OUT, R), dtype=jnp.float32) * 0.02
        return {'x': x, 'labeler_index': labeler_index, 'W': W, 'lora_A': lora_A, 'lora_B_w': lora_B_w}
    _L0_cond_all = _L0_cond_setup()
    _L0_cond_in = {k: v for k, v in _L0_cond_all.items() if k in ('W', 'lora_A', 'lora_B_w')}
    del _L0_cond_all

    def _L1_cond_setup():
        import math
        import jax, jax.numpy as jnp
        import numpy as np
        B, H, N, L = (16, 32, 64, 512)
        DT_MIN, DT_MAX = (0.001, 0.1)

        def _get_kernel(log_dt, C, log_A_real, A_imag, length):
            dt = jnp.exp(log_dt)
            Cc = C[..., 0] + 1j * C[..., 1]
            A = -jnp.exp(log_A_real) + 1j * A_imag
            dtA = A * dt[:, None]
            Ct = Cc * (jnp.exp(dtA) - 1.0) / A
            P = dtA[:, :, None] * jnp.arange(length, dtype=jnp.float32)
            K = 2.0 * jnp.einsum('hn,hnl->hl', Ct, jnp.exp(P)).real
            return K
        key = jax.random.key(seed)
        ks = jax.random.split(key, 5)
        u = jax.random.normal(ks[0], (B, H, L), dtype=jnp.float32)
        log_dt = jax.random.uniform(ks[1], (H,), dtype=jnp.float32) * (math.log(DT_MAX) - math.log(DT_MIN)) + math.log(DT_MIN)
        C = jax.random.normal(ks[2], (H, N, 2), dtype=jnp.float32)
        log_A_real = jnp.log(0.5 * jnp.ones((H, N), dtype=jnp.float32))
        A_imag = math.pi * jnp.broadcast_to(jnp.arange(N, dtype=jnp.float32), (H, N))
        D = jax.random.normal(ks[3], (H,), dtype=jnp.float32)
        length = jax.random.randint(ks[4], (B,), 1, L + 1, dtype=jnp.int32)
        return {'u': u, 'log_dt': log_dt, 'C': C, 'log_A_real': log_A_real, 'A_imag': A_imag, 'D': D, 'length': length}
    _L1_cond_all = _L1_cond_setup()
    _L1_cond_in = {k: v for k, v in _L1_cond_all.items() if k in ('log_dt', 'C', 'log_A_real', 'A_imag', 'D')}
    del _L1_cond_all
    return {'x': x, 'itok_B_0_2': itok_B_0_2, 'itok_B_78_3631': itok_B_78_3631, 'L0_cond_W': _L0_cond_in['W'], 'L0_cond_lora_A': _L0_cond_in['lora_A'], 'L0_cond_lora_B_w': _L0_cond_in['lora_B_w'], 'L1_cond_log_dt': _L1_cond_in['log_dt'], 'L1_cond_C': _L1_cond_in['C'], 'L1_cond_log_A_real': _L1_cond_in['log_A_real'], 'L1_cond_A_imag': _L1_cond_in['A_imag'], 'L1_cond_D': _L1_cond_in['D']}

def reference(x, itok_B_0_2, itok_B_78_3631, L0_cond_W, L0_cond_lora_A, L0_cond_lora_B_w, L1_cond_log_dt, L1_cond_C, L1_cond_log_A_real, L1_cond_A_imag, L1_cond_D):
    import jax
    import jax.numpy as jnp

    def _L0_cond_ref(x, labeler_index, W, lora_A, lora_B_w):
        import jax, jax.numpy as jnp
        import numpy as np
        B, S, D_IN, D_OUT = (4, 256, 512, 512)
        R, NUM_LABELERS = (32, 5)
        LORA_SCALING = 16 / 32
        base = jnp.einsum('bsi,oi->bso', x, W)
        labelers_A = lora_A[labeler_index]
        low = jnp.einsum('bsi,bir->bsr', x, labelers_A)
        delta = jnp.einsum('bsr,or->bso', low, lora_B_w) * LORA_SCALING
        return base + delta

    def _L1_cond_ref(u, log_dt, C, log_A_real, A_imag, D, length):
        import math
        import jax, jax.numpy as jnp
        import numpy as np
        B, H, N, L = (16, 32, 64, 512)
        DT_MIN, DT_MAX = (0.001, 0.1)

        def _get_kernel(log_dt, C, log_A_real, A_imag, length):
            dt = jnp.exp(log_dt)
            Cc = C[..., 0] + 1j * C[..., 1]
            A = -jnp.exp(log_A_real) + 1j * A_imag
            dtA = A * dt[:, None]
            Ct = Cc * (jnp.exp(dtA) - 1.0) / A
            P = dtA[:, :, None] * jnp.arange(length, dtype=jnp.float32)
            K = 2.0 * jnp.einsum('hn,hnl->hl', Ct, jnp.exp(P)).real
            return K
        Bq, Hq, Lq = u.shape
        K = _get_kernel(log_dt, C, log_A_real, A_imag, Lq)
        n = 2 * Lq
        kf = jnp.fft.rfft(K, n=n)
        uf = jnp.fft.rfft(u, n=n)
        y = jnp.fft.irfft(uf * kf[None], n=n)[..., :Lq]
        y = y + u * D[:, None]
        mask = (jnp.arange(Lq)[None, :] < length[:, None]).astype(u.dtype)
        return y * mask[:, None, :]
    x = x + _L0_cond_ref(x, itok_B_0_2, L0_cond_W, L0_cond_lora_A, L0_cond_lora_B_w)
    x = x + _L1_cond_ref(x, L1_cond_log_dt, L1_cond_C, L1_cond_log_A_real, L1_cond_A_imag, L1_cond_D, itok_B_78_3631)
    return x

_drawn_inputs = setup_inputs


def setup_inputs(seed=0):
    import zlib

    import numpy as np

    out = dict(_drawn_inputs(seed))
    spreads = {'L1_cond_log_A_real': (-0.6931471824645996, 0.2)}
    factors = {}
    for name, (base, spread) in spreads.items():
        noise = np.random.default_rng([zlib.crc32(name.encode()), seed]).standard_normal(out[name].shape)
        drawn = base * np.exp(spread * noise) if base else spread * noise
        out[name] = jnp.asarray(drawn.astype(out[name].dtype))
    for name, factor in factors.items():
        out[name] = (out[name] * factor).astype(out[name].dtype)
    return out
```

```python
from contextlib import ExitStack
import math

import concourse.bass as bass
from concourse import mybir

F32 = mybir.dt.float32
F32R = mybir.dt.float32r
I32 = mybir.dt.int32
ALU = mybir.AluOpType
ACT = mybir.ActivationFunctionType
AX = mybir.AxisListType

P = 128
H = 32
L = 512
CH = L // P
NLAB = 5
RANK = 32
LOW = NLAB * RANK
LORA_SCALING = 0.5
NST = 64
LB = 32
LA = L // LB
HG = P // LA
NG = H // HG
PADK = P + L
TR = 4
XG = 4

ACT_KGEN_HEAD = 12
DVE_KGEN_HEAD = 16
PE_KGEN_HEAD = 22
T_HEAD = H - TR + 1

ROUND = 1.5 * 2.0 ** 23
LN2_HI = 0.693145751953125
LN2_LO = 1.42860682030941723e-6


def conditioned_residual(nc, x, lab, length, w_t, lora_a, lora_bt, log_dt, ssm, d_skip, out):
    ctx = ExitStack()
    with ctx:
        def sb(name, shape, dt=F32):
            return ctx.enter_context(nc.sbuf_tensor(name, shape, dt))

        def ps(name, shape):
            return ctx.enter_context(nc.psum_tensor(name, shape, F32))

        def sem(name):
            return ctx.enter_context(nc.semaphore(name))

        x_all = sb("x_all", [P, H, L])
        x_slot = sb("x_slot", [P, TR, L])
        xt_hi = sb("xt_hi", [P, 2, CH, P], F32R)
        xt_lo = sb("xt_lo", [P, 2, CH, P], F32R)
        w_raw = sb("w_raw", [P, CH, L])
        w_hi = sb("w_hi", [P, CH, L], F32R)
        w_lo = sb("w_lo", [P, CH, L], F32R)
        a_raw = sb("a_raw", [P, CH, LOW])
        a_hi = sb("a_hi", [P, CH, LOW], F32R)
        a_lo = sb("a_lo", [P, CH, LOW], F32R)
        b_raw = sb("b_raw", [3 * RANK, L])
        b_stack = sb("b_stack", [3 * RANK, L], F32R)
        low_stack = sb("low_stack", [3 * RANK, 2, P], F32R)
        waited = sb("waited", [1, TR])
        low_prod = sb("low_prod", [P, LOW])
        low_sel = sb("low_sel", [P, 2, RANK])
        ident = sb("ident", [P, P])
        lab_i = sb("lab_i", [P, 1], I32)
        len_i = sb("len_i", [P, 1], I32)
        lab_f = sb("lab_f", [P, 1])
        lab_neg = sb("lab_neg", [P, 1])
        len_f = sb("len_f", [P, 1])
        lab_iota = sb("lab_iota", [P, NLAB, RANK])
        lab_mask = sb("lab_mask", [P, NLAB, RANK])
        l_iota = sb("l_iota", [P, L])
        len_mask = sb("len_mask", [P, L], I32)
        logs = sb("logs", [P, 2, H])
        prm = sb("prm", [P, 3, H])
        d_row = sb("d_row", [1, H])
        ex = sb("ex", [P, 2, H])
        e_k = sb("e_k", [P, 2, H])
        e_r = sb("e_r", [P, 2, H])
        e_p = sb("e_p", [P, 2, H])
        e_i = sb("e_i", [P, 2, H], I32)
        half_a = sb("half_a", [P, H])
        re_dta = sb("re_dta", [P, H])
        turns = sb("turns", [P, H])
        tmp = sb("tmp", [P, 12, H])
        recip = sb("recip", [P, H])
        ramp_b = sb("ramp_b", [P, LB])
        ramp_a = sb("ramp_a", [P, LA])
        shift = sb("shift", [P, 2])
        sign = sb("sign", [P, 1])
        NQ, NP = H * LB, H * LA
        phase = sb("phase", [P, NQ + 2 * NP + 2 * H])
        whole = sb("whole", [P, NQ + 2 * NP + 2 * H])
        mag = sb("mag", [P, NQ + NP])
        k_d = sb("k_d", [1, H, LA])
        k_one = sb("k_one", [1, HG, LB])
        k_sb = sb("k_sb", [P, NG, HG * LB])
        zeros = sb("zeros", [H, P])
        t_raw = sb("t_raw", [P, TR, L])
        t_hi = sb("t_hi", [P, TR, L], F32R)
        t_lo = sb("t_lo", [P, TR, L], F32R)
        k_pad = nc.dram_tensor("k_pad", (H, PADK), F32).ap()

        xt_ps = [ps(f"xt_ps{i}", [P, CH, P]) for i in range(2)]
        y_ps = [ps(f"y_ps{i}", [P, L]) for i in range(2)]
        low_ps = ps("low_ps", [P, L])
        lowt_ps = ps("lowt_ps", [P, L])
        k_ps = ps("k_ps", [P, NG, HG * LB])

        x_load = [sem(f"x_load{i}") for i in range(2)]
        x_here = sem("x_here")
        w_load = sem("w_load")
        a_load = sem("a_load")
        b_load = sem("b_load")
        idx_load = sem("idx_load")
        prm_load = sem("prm_load")
        t_load = [sem(f"t_load{i}") for i in range(TR)]
        k_stored = sem("k_stored")
        zeros_stored = sem("zeros_stored")
        out_stored = [sem(f"out_stored{i}") for i in range(TR)]
        consts = sem("consts")
        ident_zero = sem("ident_zero")
        w_split = sem("w_split")
        a_split = sem("a_split")
        b_split = sem("b_split")
        hi_done = sem("hi_done")
        dve_own = sem("dve_own")
        masks = sem("masks")
        slot_full = sem("slot_full")
        xt_done = sem("xt_done")
        xt_hi_done = sem("xt_hi_done")
        xt_lo_done = sem("xt_lo_done")
        low_done = sem("low_done")
        low_read = sem("low_read")
        sel_done = sem("sel_done")
        lowt_done = sem("lowt_done")
        lowst_hi = sem("lowst_hi")
        lowst_done = sem("lowst_done")
        y_done = sem("y_done")
        y_read = sem("y_read")
        pool_own = sem("pool_own")
        k_args = sem("k_args")
        k_funcs = sem("k_funcs")
        k_den = sem("k_den")
        k_recip = sem("k_recip")
        k_factors = sem("k_factors")
        k_product = sem("k_product")
        k_out = sem("k_out")
        t_hi_done = sem("t_hi_done")
        t_lo_done = sem("t_lo_done")

        block = ctx.enter_context(nc.Block())

        def f32(ap):
            return ap.bitcast(F32)

        @block.sync
        def _(sp):
            def load_x(n):
                sp.dma_start(x_all[:, XG * n:XG * n + XG, :],
                             x[:, XG * n:XG * n + XG, :]).then_inc(x_load[n % 2], 16)

            def x_arrived(n):
                sp.wait_ge(x_load[n % 2], 16 * (n // 2 + 1))
                sp.nop().then_inc(x_here, XG)

            load_x(0)
            sp.dma_start(w_raw[:], w_t.rearrange("(c p) o -> p c o", p=P)).then_inc(w_load, 16)
            sp.dma_start(a_raw[:], lora_a.rearrange("(c p) r -> p c r", p=P)).then_inc(a_load, 16)
            load_x(1)
            for n in range(H // XG):
                x_arrived(n)
                if n + 2 < H // XG:
                    load_x(n + 2)

            sp.wait_ge(k_out, 1)
            for j in range(HG):
                rows = k_pad[j:H:HG, 0:L].rearrange("g (a b) -> a g b", b=LB)
                sp.dma_start(rows, k_sb[LA * j:LA * j + LA, :, LB * j:LB * j + LB]).then_inc(k_stored, 16)
            sp.wait_ge(k_stored, 16 * HG)
            sp.wait_ge(zeros_stored, 16)

            def load_t(k, slot):
                window = bass.AP(k_pad.tensor, k * PADK, [[1, P], [1, L]])
                sp.dma_start(t_raw[:, slot, :], window).then_inc(t_load[slot], 16)

            def store(h, slot):
                sp.wait_ge(y_read, h + H + 1)
                sp.dma_start(out[:, bass.ds(h, 1), :], x_slot[:, slot:slot + 1, :]).then_inc(out_stored[slot], 16)

            for k in range(TR):
                load_t(k, k)
            with sp.Fori(0, H // TR - 1) as turn:
                for u in range(TR):
                    h = turn * TR + u
                    sp.wait_ge(t_lo_done, h + 1)
                    load_t(h + TR, u)
                    store(h, u)
            for h in range(H - TR, H):
                store(h, h % TR)
            for slot in range(TR):
                sp.wait_ge(out_stored[slot], 16 * (H // TR))

        @block.gpsimd
        def _(pool):
            own = [0]

            def step(ins):
                own[0] += 1
                ins.then_inc(pool_own, 1)
                pool.wait_ge(pool_own, own[0])

            g = nc.gpsimd
            g.dma_start(lab_i[:], lab.rearrange("(p o) -> p o", o=1)).then_inc(idx_load, 16)
            g.dma_start(len_i[:], length.rearrange("(p o) -> p o", o=1)).then_inc(idx_load, 16)
            g.memset(ident[:], 0.0).then_inc(ident_zero, 1)
            g.iota(lab_iota[:], pattern=[[1, NLAB], [0, RANK]], base=0, channel_multiplier=0,
                   allow_small_or_imprecise_dtypes=True).then_inc(consts, 1)
            pool.wait_ge(ident_zero, 1)
            g.affine_select(out=ident[:], in_=ident[:], compare_op=ALU.not_equal, fill=1.0, base=0,
                            pattern=[[-1, P]], channel_multiplier=1).then_inc(consts, 1)
            g.iota(l_iota[:], pattern=[[1, L]], base=0, channel_multiplier=0,
                   allow_small_or_imprecise_dtypes=True).then_inc(consts, 1)
            for half in range(2):
                rows = slice(NST * half, NST * half + NST)
                g.dma_start(logs[rows, 1, :], ssm[:, 0, :]).then_inc(prm_load, 16)
                g.dma_start(prm[rows, :, :], ssm[:, 1:4, :]).then_inc(prm_load, 16)
            g.dma_start(logs[:, 0, :], log_dt.rearrange("(o h) -> o h", o=1).broadcast_to([P, H]))\
                .then_inc(prm_load, 16)
            g.dma_start(d_row[:], d_skip.rearrange("(o h) -> o h", o=1)).then_inc(prm_load, 16)
            step(g.memset(zeros[:], 0.0))
            g.dma_start(k_pad[:, L:PADK], zeros[:]).then_inc(zeros_stored, 16)
            step(g.iota(ramp_b[:], pattern=[[-1, LB]], base=LB - 1, channel_multiplier=0,
                        allow_small_or_imprecise_dtypes=True))
            step(g.iota(ramp_a[:], pattern=[[-LB, LA]], base=LB * (LA - 1), channel_multiplier=0,
                        allow_small_or_imprecise_dtypes=True))
            step(g.memset(shift[:], 0.0))
            step(g.memset(shift[0:NST, 0:1], 0.25))
            step(g.memset(shift[NST:P, 1:2], 0.25))
            step(g.memset(sign[0:NST, :], 1.0))
            step(g.memset(sign[NST:P, :], -1.0))
            step(g.memset(k_d[:], 0.0))
            step(g.memset(k_one[:], 0.0))
            step(g.memset(k_one[:, :, LB - 1:LB], 1.0))
            pool.wait_ge(prm_load, 16 * 6)

            def ts(o, i, s1, s2, op0, op1):
                step(g.tensor_scalar(o, i, s1, s2, op0, op1))

            def tt(o, a, b, op):
                step(g.tensor_tensor(o, a, b, op))

            ts(k_d[:, :, LA - 1], d_row[:], 1.0, 1.0, ALU.add, ALU.mult)
            ts(logs[:], logs[:], -87.0, 88.0, ALU.max, ALU.min)
            ts(e_k[:], logs[:], 1.0 / math.log(2.0), ROUND, ALU.mult, ALU.add)
            ts(e_k[:], e_k[:], 1.0, -ROUND, ALU.mult, ALU.add)
            ts(e_p[:], e_k[:], -LN2_HI, 0.0, ALU.mult, ALU.add)
            tt(e_r[:], logs[:], e_p[:], ALU.add)
            ts(e_p[:], e_k[:], -LN2_LO, 0.0, ALU.mult, ALU.add)
            tt(e_r[:], e_r[:], e_p[:], ALU.add)
            ts(e_p[:], e_r[:], 1.0 / math.factorial(7), 1.0 / math.factorial(6), ALU.mult, ALU.add)
            for n in range(5, -1, -1):
                tt(e_p[:], e_p[:], e_r[:], ALU.mult)
                ts(e_p[:], e_p[:], 1.0, 1.0 / math.factorial(n), ALU.mult, ALU.add)
            ts(e_i[:], e_k[:], 127.0, float(2 ** 23), ALU.add, ALU.mult)
            tt(ex[:], e_p[:], e_i[:].bitcast(F32), ALU.mult)
            dt, neg_re = ex[:, 0, :], ex[:, 1, :]
            a_im, c_re, c_im = prm[:, 0, :], prm[:, 1, :], prm[:, 2, :]
            tt(re_dta[:], dt, neg_re, ALU.mult)
            ts(re_dta[:], re_dta[:], -1.0, 0.0, ALU.mult, ALU.add)
            ts(half_a[:], re_dta[:], 0.5, 0.0, ALU.mult, ALU.add)
            tt(turns[:], a_im, dt, ALU.mult)
            ts(turns[:], turns[:], 1.0 / (2.0 * math.pi), 0.0, ALU.mult, ALU.add)

            def outer(o, v, ramp, n):
                tt(o.rearrange("p (h n) -> p h n", n=n), v.unsqueeze(2).to_broadcast([P, H, n]),
                   ramp.unsqueeze(1).to_broadcast([P, H, n]), ALU.mult)

            q_at, u_at, v_at, s_at = 0, NQ, NQ + NP, NQ + 2 * NP
            outer(phase[:, q_at:u_at], turns[:], ramp_b[:], LB)
            outer(phase[:, u_at:v_at], turns[:], ramp_a[:], LA)
            ts(phase[:, v_at:s_at], phase[:, u_at:v_at], shift[:, 1:2], 1.0, ALU.add, ALU.mult)
            ts(phase[:, q_at:v_at], phase[:, q_at:v_at], shift[:, 0:1], 1.0, ALU.add, ALU.mult)
            ts(phase[:, s_at:s_at + H], turns[:], 0.5, 0.0, ALU.mult, ALU.add)
            ts(phase[:, s_at + H:], turns[:], 1.0, 0.0, ALU.mult, ALU.add)
            ts(whole[:], phase[:], 1.0, ROUND, ALU.mult, ALU.add)
            ts(whole[:], whole[:], 1.0, -ROUND, ALU.mult, ALU.add)
            tt(phase[:], phase[:], whole[:], ALU.subtract)
            outer(mag[:, 0:NQ], re_dta[:], ramp_b[:], LB)
            outer(mag[:, NQ:NQ + NP], re_dta[:], ramp_a[:], LA)
            g.nop().then_inc(k_args, 1)

            pool.wait_ge(k_funcs, 3)
            tanh, sin_half, sin_one = half_a[:], phase[:, s_at:s_at + H], phase[:, s_at + H:]
            q = phase[:, q_at:u_at]
            u, v = phase[:, u_at:v_at], phase[:, v_at:s_at]
            T = [tmp[:, i, :] for i in range(12)]
            tt(T[0], neg_re, neg_re, ALU.mult)
            tt(T[1], a_im, a_im, ALU.mult)
            tt(T[0], T[0], T[1], ALU.add)
            ts(T[1], tanh, -1.0, 1.0, ALU.mult, ALU.add)
            own[0] += 1
            g.tensor_tensor(T[2], T[0], T[1], ALU.mult).then_inc(pool_own, 1)
            pool.wait_ge(pool_own, own[0])
            g.nop().then_inc(k_den, 1)
            ts(T[3], tanh, 1.0, 0.0, ALU.add, ALU.add)
            tt(T[4], sin_half, sin_half, ALU.mult)
            tt(T[4], T[4], T[3], ALU.mult)
            tt(T[4], tanh, T[4], ALU.subtract)
            ts(T[4], T[4], 2.0, 0.0, ALU.mult, ALU.add)
            tt(T[5], T[3], sin_one, ALU.mult)
            tt(T[6], T[5], a_im, ALU.mult)
            tt(T[7], T[4], neg_re, ALU.mult)
            tt(T[6], T[6], T[7], ALU.subtract)
            tt(T[7], T[5], neg_re, ALU.mult)
            tt(T[8], T[4], a_im, ALU.mult)
            tt(T[7], T[7], T[8], ALU.add)
            tt(T[8], c_re, T[6], ALU.mult)
            tt(T[9], c_im, T[7], ALU.mult)
            tt(T[9], T[8], T[9], ALU.add)
            tt(T[8], c_re, T[7], ALU.mult)
            tt(T[10], c_im, T[6], ALU.mult)
            tt(T[10], T[8], T[10], ALU.subtract)
            pool.wait_ge(k_recip, 1)
            ts(recip[:], recip[:], 2.0, 0.0, ALU.mult, ALU.add)
            tt(T[9], T[9], recip[:], ALU.mult)
            ts(T[9], T[9], sign[:], 1.0, ALU.mult, ALU.mult)
            tt(T[10], T[10], recip[:], ALU.mult)
            tt(q, q, mag[:, 0:NQ], ALU.mult)
            tt(u, u, mag[:, NQ:NQ + NP], ALU.mult)
            tt(v, v, mag[:, NQ:NQ + NP], ALU.mult)

            def by_head(o, i, c):
                tt(o.rearrange("p (h n) -> p h n", n=LA), i.rearrange("p (h n) -> p h n", n=LA),
                   c.unsqueeze(2).to_broadcast([P, H, LA]), ALU.mult)

            by_head(u, u, T[9])
            by_head(v, v, T[10])
            own[0] += 1
            g.tensor_tensor(u, u, v, ALU.add).then_inc(pool_own, 1)
            pool.wait_ge(pool_own, own[0])
            g.nop().then_inc(k_factors, 1)

            def split_t(k, slot):
                pool.wait_ge(t_hi_done, k + 1)
                g.tensor_tensor(t_lo[:, slot, :], t_raw[:, slot, :], f32(t_hi[:, slot, :]),
                                ALU.subtract).then_inc(t_lo_done, 1)

            with pool.Fori(0, H // TR) as turn:
                for slot in range(TR):
                    split_t(turn * TR + slot, slot)

        @block.scalar
        def _(act):
            s = nc.scalar

            act.dma_start(b_raw[0:RANK, :], lora_bt).then_inc(b_load, 16)
            act.dma_start(b_raw[RANK:2 * RANK, :], lora_bt).then_inc(b_load, 16)
            act.dma_start(b_raw[2 * RANK:3 * RANK, :], lora_bt).then_inc(b_load, 16)

            def fill_slot(slot, head):
                s.copy(x_slot[:, slot, :], x_all[:, head, :] if isinstance(head, int)
                       else x_all[:, bass.ds(head, 1), :]).then_inc(slot_full, 1)

            def split_xt_hi(step, slot):
                act.wait_ge(xt_done, step + 1)
                s.copy(xt_hi[:, slot, :, :], xt_ps[slot][:]).then_inc(xt_hi_done, 1)

            def split_t_hi(k, slot, turn):
                act.wait_ge(t_load[slot], 16 * (turn + 1))
                s.copy(t_hi[:, slot, :], t_raw[:, slot, :]).then_inc(t_hi_done, 1)

            act.wait_ge(x_here, 2)
            fill_slot(0, 0)
            fill_slot(1, 1)
            act.wait_ge(a_load, 16)
            s.copy(a_hi[:], a_raw[:]).then_inc(hi_done, 1)
            split_xt_hi(0, 0)
            act.wait_ge(w_load, 16)
            s.copy(w_hi[:], w_raw[:]).then_inc(hi_done, 1)
            act.wait_ge(b_load, 48)
            s.mul(b_stack[:], b_raw[:], LORA_SCALING).then_inc(hi_done, 1)

            def pass1(h, p, nxt):
                if not (isinstance(h, int) and h == 0):
                    act.wait_ge(y_done, h)
                split_xt_hi(h + 1, 1 - p)
                if nxt is None:
                    act.wait_ge(x_here, h + 3)
                    fill_slot(p, h + 2)
                else:
                    act.wait_ge(y_read, nxt + 1)
                    fill_slot(p, nxt)
                act.wait_ge(lowt_done, h + 1)
                s.copy(low_stack[0:RANK, p, :], lowt_ps[0:RANK, 0:P]).then_inc(lowst_hi, 1)
                s.copy(low_stack[2 * RANK:3 * RANK, p, :], lowt_ps[0:RANK, 0:P]).then_inc(lowst_hi, 1)

            def heads(first, last):
                with act.Fori(first // 2, last // 2) as pair:
                    for u in range(2):
                        pass1(pair * 2 + u, u, None)

            pass1(0, 0, None)
            pass1(1, 1, None)
            heads(2, ACT_KGEN_HEAD)
            act.wait_ge(k_args, 1)
            s.activation(half_a[:], half_a[:], ACT.Tanh).then_inc(k_funcs, 1)
            s.activation(mag[:], mag[:], ACT.Exp).then_inc(k_funcs, 1)
            pass1(ACT_KGEN_HEAD, 0, None)
            pass1(ACT_KGEN_HEAD + 1, 1, None)
            s.activation(phase[:], phase[:], ACT.Sin, scale=2.0 * math.pi).then_inc(k_funcs, 1)
            heads(ACT_KGEN_HEAD + 2, PE_KGEN_HEAD)
            act.wait_ge(k_product, 1)
            s.copy(k_sb[:], k_ps[:]).then_inc(k_out, 1)
            heads(PE_KGEN_HEAD, T_HEAD - 1)
            for h in range(T_HEAD - 1, H):
                pass1(h, h % 2, None if h + 2 < H else h + 2 - H)
                if h >= T_HEAD:
                    split_t_hi(h - T_HEAD, h - T_HEAD, 0)

            def pass2(h, u, turn, first=False, last=False):
                if not (isinstance(h, int) and h == H - 1):
                    act.wait_ge(y_done, h + H)
                    split_xt_hi(h + H + 1, (u + 1) % 2)
                if not last or h + 2 < H:
                    if u < 2:
                        if not first:
                            act.wait_ge(out_stored[u + 2], turn * 16)
                    else:
                        act.wait_ge(out_stored[u - 2], (turn + 1) * 16)
                    fill_slot((u + 2) % TR, h + 2)
                if not last or h + TR - 1 < H:
                    split_t_hi(h + TR - 1, (u + TR - 1) % TR, turn if u == 0 else turn + 1)

            for h in range(TR):
                pass2(h, h, 0, first=True)
            with act.Fori(1, H // TR - 1) as turn:
                for u in range(TR):
                    pass2(turn * TR + u, u, turn)
            for h in range(H - TR, H):
                pass2(h, h % TR, H // TR - 1, last=True)

        @block.tensor
        def _(pe):
            mm = nc.tensor.matmul

            def transposes(step, slot, ring):
                pe.wait_ge(slot_full, step + 1)
                if not (isinstance(step, int) and step < 2):
                    pe.wait_ge(xt_lo_done, step - 1)
                for c in range(CH):
                    last = nc.tensor.transpose(xt_ps[slot][:, c, :], x_slot[:, ring, c * P:(c + 1) * P],
                                               ident[:])
                last.then_inc(xt_done, 1)

            def pass1(h, p):
                first = isinstance(h, int) and h == 0
                transposes(h + 1, 1 - p, 1 - p)
                pe.wait_ge(xt_hi_done, h + 1)
                pe.wait_ge(xt_lo_done, h + 1)
                if first:
                    pe.wait_ge(a_split, 1)
                else:
                    pe.wait_ge(low_read, h)
                for c in range(CH):
                    mm(low_ps[:, 0:LOW], xt_hi[:, p, c, :], a_hi[:, c, :], start=(c == 0), stop=False)
                    mm(low_ps[:, 0:LOW], xt_hi[:, p, c, :], a_lo[:, c, :], start=False, stop=False)
                    last = mm(low_ps[:, 0:LOW], xt_lo[:, p, c, :], a_hi[:, c, :], start=False,
                              stop=(c == CH - 1))
                last.then_inc(low_done, 1)
                if first:
                    pe.wait_ge(w_split, 1)
                if not (isinstance(h, int) and h < 2):
                    pe.wait_ge(y_read, h - 1)
                for c in range(CH):
                    if c == CH // 2:
                        pe.wait_ge(sel_done, h + 1)
                        if not first:
                            pe.wait_ge(lowst_done, h)
                        nc.tensor.transpose(lowt_ps[0:RANK, 0:P], low_sel[:, p, :], ident[:])\
                            .then_inc(lowt_done, 1)
                    mm(y_ps[p][:], xt_hi[:, p, c, :], w_hi[:, c, :], start=(c == 0), stop=False)
                    mm(y_ps[p][:], xt_hi[:, p, c, :], w_lo[:, c, :], start=False, stop=False)
                    mm(y_ps[p][:], xt_lo[:, p, c, :], w_hi[:, c, :], start=False, stop=False)
                pe.wait_ge(lowst_done, h + 1)
                if first:
                    pe.wait_ge(b_split, 1)
                mm(y_ps[p][:], low_stack[:, p, :], b_stack[:], start=False, stop=True).then_inc(y_done, 1)

            def heads(first, last):
                with pe.Fori(first // 2, last // 2) as pair:
                    for u in range(2):
                        pass1(pair * 2 + u, u)

            pe.wait_ge(consts, 3)
            transposes(0, 0, 0)
            pass1(0, 0)
            pass1(1, 1)
            heads(2, PE_KGEN_HEAD)
            pe.wait_ge(k_factors, 1)
            for g in range(NG):
                pq = phase[:, NQ + g * HG * LA:NQ + (g + 1) * HG * LA]
                mm(k_ps[:, g, :], pq, phase[:, g * HG * LB:(g + 1) * HG * LB], start=True, stop=False)
                last = mm(k_ps[:, g, :], k_d[:, g * HG:(g + 1) * HG, :].rearrange("o h a -> o (h a)"),
                          k_one[:].rearrange("o h b -> o (h b)"), start=False, stop=True)
            last.then_inc(k_product, 1)
            heads(PE_KGEN_HEAD, H)

            def pass2(h, u, more=True):
                p = u % 2
                if more:
                    transposes(h + H + 1, 1 - p, (u + 1) % TR)
                pe.wait_ge(xt_hi_done, h + H + 1)
                pe.wait_ge(xt_lo_done, h + H + 1)
                pe.wait_ge(t_hi_done, h + 1)
                pe.wait_ge(t_lo_done, h + 1)
                pe.wait_ge(y_read, h + H - 1)
                for c in range(CH):
                    o, t = y_ps[p][:, 0:L - c * P], slice(c * P, L)
                    mm(o, xt_hi[:, p, c, :], t_hi[:, u, t], start=(c == 0), stop=False)
                    mm(o, xt_hi[:, p, c, :], t_lo[:, u, t], start=False, stop=False)
                    last = mm(o, xt_lo[:, p, c, :], t_hi[:, u, t], start=False, stop=(c == CH - 1))
                last.then_inc(y_done, 1)

            with pe.Fori(0, H // TR - 1) as turn:
                for u in range(TR):
                    pass2(turn * TR + u, u)
            for h in range(H - TR, H):
                pass2(h, h % TR, more=(h < H - 1))

        @block.vector
        def _(dve):
            v = nc.vector
            own = [0]

            def step(ins):
                own[0] += 1
                ins.then_inc(dve_own, 1)
                dve.wait_ge(dve_own, own[0])

            def split_xt_lo(st, slot):
                dve.wait_ge(xt_hi_done, st + 1)
                v.tensor_tensor(xt_lo[:, slot, :, :], xt_ps[slot][:], f32(xt_hi[:, slot, :, :]),
                                ALU.subtract).then_inc(xt_lo_done, 1)

            dve.wait_ge(idx_load, 32)
            step(v.tensor_copy(lab_f[:], lab_i[:]))
            step(v.tensor_copy(len_f[:], len_i[:]))
            step(v.tensor_scalar(lab_neg[:], lab_f[:], 0.0, float(NLAB), ALU.is_lt, ALU.mult))
            step(v.tensor_tensor(lab_f[:], lab_f[:], lab_neg[:], ALU.add))
            step(v.tensor_scalar(lab_f[:], lab_f[:], 0.0, float(NLAB - 1), ALU.max, ALU.min))
            dve.wait_ge(consts, 3)
            v.tensor_scalar(lab_mask[:], lab_iota[:], lab_f[:], None, ALU.is_equal).then_inc(masks, 1)
            v.tensor_scalar(len_mask[:], l_iota[:], len_f[:], None, ALU.is_lt).then_inc(masks, 1)
            dve.wait_ge(hi_done, 1)
            v.tensor_tensor(a_lo[:], a_raw[:], f32(a_hi[:]), ALU.subtract).then_inc(a_split, 1)
            split_xt_lo(0, 0)
            dve.wait_ge(hi_done, 2)
            v.tensor_tensor(w_lo[:], w_raw[:], f32(w_hi[:]), ALU.subtract).then_inc(w_split, 1)
            dve.wait_ge(hi_done, 3)
            lo = slice(2 * RANK, 3 * RANK)
            v.scalar_tensor_tensor(b_stack[lo, :], b_raw[lo, :], LORA_SCALING, f32(b_stack[lo, :]),
                                   ALU.mult, ALU.subtract).then_inc(b_split, 1)
            dve.wait_ge(masks, 1)

            def pass1(h, p):
                dve.wait_ge(low_done, h + 1)
                v.tensor_tensor(low_prod[:], low_ps[:, 0:LOW], lab_mask[:].rearrange("p l r -> p (l r)"),
                                ALU.mult).then_inc(low_read, 1)
                dve.wait_ge(low_read, h + 1)
                v.tensor_reduce(low_sel[:, p, :], low_prod[:].rearrange("p (l r) -> p r l", l=NLAB),
                                AX.X, ALU.add).then_inc(sel_done, 1)
                split_xt_lo(h + 1, 1 - p)
                dve.wait_ge(lowst_hi, 2 * h + 2)
                v.tensor_tensor(low_stack[RANK:2 * RANK, p, :], lowt_ps[0:RANK, 0:P],
                                f32(low_stack[0:RANK, p, :]), ALU.subtract).then_inc(lowst_done, 1)
                dve.wait_ge(y_done, h + 1)
                xh = x_all[:, h, :] if isinstance(h, int) else x_all[:, bass.ds(h, 1), :]
                y = y_ps[p][:] if isinstance(h, int) else y_ps[p][:].unsqueeze(1)
                v.tensor_tensor(xh, y, xh, ALU.add).then_inc(y_read, 1)

            def heads(first, last):
                with dve.Fori(first // 2, last // 2) as pair:
                    for u in range(2):
                        pass1(pair * 2 + u, u)

            heads(0, DVE_KGEN_HEAD)
            dve.wait_ge(k_den, 1)
            v.reciprocal(recip[:], tmp[:, 2, :]).then_inc(k_recip, 1)
            heads(DVE_KGEN_HEAD, H)

            def pass2(h, u, more=True):
                if more:
                    split_xt_lo(h + H + 1, (u + 1) % 2)
                dve.wait_ge(y_done, h + H + 1)
                v.memset(waited[:, u:u + 1], 0.0)
                dve.wait_ge(masks, 2)
                v.copy_predicated(x_slot[:, u, :], len_mask[:], y_ps[u % 2][:, ::-1]).then_inc(y_read, 1)

            with dve.Fori(0, H // TR - 1) as turn:
                for u in range(TR):
                    pass2(turn * TR + u, u)
            for h in range(H - TR, H):
                pass2(h, h % TR, more=(h < H - 1))


def kernel(x, itok_B_0_2, itok_B_78_3631, L0_cond_W, L0_cond_lora_A, L0_cond_lora_B_w,
           L1_cond_log_dt, L1_cond_C, L1_cond_log_A_real, L1_cond_A_imag, L1_cond_D):
    import numpy as np
    import concourse.bacc as bacc
    from concourse.bass_utils import run_bass_kernel_spmd

    C = np.asarray(L1_cond_C)
    ssm = np.stack([np.asarray(L1_cond_log_A_real).T, np.asarray(L1_cond_A_imag).T,
                    C[:, :, 0].T, C[:, :, 1].T], axis=1)
    arrays = {
        "x": np.asarray(x),
        "lab": np.asarray(itok_B_0_2),
        "length": np.asarray(itok_B_78_3631),
        "w_t": np.asarray(L0_cond_W).T,
        "lora_a": np.asarray(L0_cond_lora_A).transpose(1, 0, 2).reshape(L, LOW),
        "lora_bt": np.asarray(L0_cond_lora_B_w).T,
        "log_dt": np.asarray(L1_cond_log_dt),
        "ssm": ssm,
        "d_skip": np.asarray(L1_cond_D),
    }
    arrays = {"in_" + k: np.ascontiguousarray(v) for k, v in arrays.items()}
    nc = bacc.Bacc("TRN2", target_bir_lowering=False, num_devices=1)
    args = [nc.dram_tensor(k, v.shape, mybir.dt.from_np(v.dtype), kind="ExternalInput").ap()
            for k, v in arrays.items()]
    out = nc.dram_tensor("out_0", (P, H, L), F32, kind="ExternalOutput").ap()
    conditioned_residual(nc, *args, out)
    r = run_bass_kernel_spmd(nc, [arrays], core_ids=[0])
    return r.results[0]["out_0"]
```

```python
from contextlib import ExitStack
import math

import concourse.bass as bass
from concourse import mybir

F32 = mybir.dt.float32
F32R = mybir.dt.float32r
I32 = mybir.dt.int32
ALU = mybir.AluOpType
ACT = mybir.ActivationFunctionType
AX = mybir.AxisListType

P = 128
H = 32
L = 512
CH = L // P
NLAB = 5
RANK = 32
LOW = NLAB * RANK
LORA_SCALING = 0.5
NST = 64
LB = 32
LA = L // LB
HG = P // LA
NG = H // HG
PADK = P + L
TR = 6
FIRST, TURNS = 4, 4
LAST = FIRST + TURNS * TR
HALF = L // 2
WA = L + LOW
XG = 4

ACT_KGEN_HEAD = 12
DVE_KGEN_HEAD = 16
PE_KGEN_HEAD = 22
T_HEAD = H - 4

ROUND = 1.5 * 2.0 ** 23
LN2_HI = 0.693145751953125
LN2_LO = 1.42860682030941723e-6


def conditioned_residual(nc, x, lab, length, wa, lora_bt, log_dt, ssm, d_skip, out):
    ctx = ExitStack()
    with ctx:
        def sb(name, shape, dt=F32):
            return ctx.enter_context(nc.sbuf_tensor(name, shape, dt))

        def ps(name, shape):
            return ctx.enter_context(nc.psum_tensor(name, shape, F32))

        def sem(name):
            return ctx.enter_context(nc.semaphore(name))

        x_all = sb("x_all", [P, H, L])
        x_slot = sb("x_slot", [P, TR, L])
        xt_hi = sb("xt_hi", [P, 2, CH, P], F32R)
        xt_lo = sb("xt_lo", [P, 2, CH, P], F32R)
        w_raw = sb("w_raw", [P, CH, WA])
        w_hi = sb("w_hi", [P, CH, WA], F32R)
        w_lo = sb("w_lo", [P, CH, WA], F32R)
        b_raw = sb("b_raw", [3 * RANK, L])
        b_stack = sb("b_stack", [3 * RANK, L], F32R)
        low_stack = sb("low_stack", [3 * RANK, 2, P], F32R)
        waited = sb("waited", [1, TR])
        low_prod = sb("low_prod", [P, LOW])
        low_sel = sb("low_sel", [P, 2, RANK])
        ident = sb("ident", [P, P])
        lab_i = sb("lab_i", [P, 1], I32)
        len_i = sb("len_i", [P, 1], I32)
        lab_f = sb("lab_f", [P, 1])
        lab_neg = sb("lab_neg", [P, 1])
        len_f = sb("len_f", [P, 1])
        lab_iota = sb("lab_iota", [P, NLAB, RANK])
        lab_mask = sb("lab_mask", [P, NLAB, RANK])
        l_iota = sb("l_iota", [P, L])
        len_mask = sb("len_mask", [P, L], I32)
        logs = sb("logs", [P, 2, H])
        prm = sb("prm", [P, 3, H])
        d_row = sb("d_row", [1, H])
        ex = sb("ex", [P, 2, H])
        e_k = sb("e_k", [P, 2, H])
        e_r = sb("e_r", [P, 2, H])
        e_p = sb("e_p", [P, 2, H])
        e_i = sb("e_i", [P, 2, H], I32)
        half_a = sb("half_a", [P, H])
        re_dta = sb("re_dta", [P, H])
        turns = sb("turns", [P, H])
        tmp = sb("tmp", [P, 12, H])
        recip = sb("recip", [P, H])
        ramp_b = sb("ramp_b", [P, LB])
        ramp_a = sb("ramp_a", [P, LA])
        shift = sb("shift", [P, 2])
        sign = sb("sign", [P, 1])
        NQ, NP = H * LB, H * LA
        phase = sb("phase", [P, NQ + 2 * NP + 2 * H])
        whole = sb("whole", [P, NQ + 2 * NP + 2 * H])
        mag = sb("mag", [P, NQ + NP])
        k_d = sb("k_d", [1, H, LA])
        k_one = sb("k_one", [1, HG, LB])
        k_sb = sb("k_sb", [P, NG, HG * LB])
        zeros = sb("zeros", [H, P])
        t_raw = sb("t_raw", [P, TR, L])
        t_hi = sb("t_hi", [P, TR, L], F32R)
        t_lo = sb("t_lo", [P, TR, L], F32R)
        k_pad = nc.dram_tensor("k_pad", (H, PADK), F32).ap()

        xt_ps = [ps(f"xt_ps{i}", [P, CH, P]) for i in range(2)]
        y_ps = [ps(f"y_ps{i}", [P, 2, L]) for i in range(2)]
        y1 = [y[:, :, 0:HALF] for y in y_ps]
        low_ps = [y[:, 1, HALF:HALF + LOW] for y in y_ps]
        y2 = [y[:, 0, :] for y in y_ps]
        lowt_ps = ps("lowt_ps", [P, L])
        k_ps = ps("k_ps", [P, NG // 2, HG * LB])

        x_load = [sem(f"x_load{i}") for i in range(2)]
        x_here = sem("x_here")
        slot_load = [sem(f"slot_load{i}") for i in range(2)]
        w_load = [sem(f"w_load{c}") for c in range(CH)]
        b_load = sem("b_load")
        idx_load = sem("idx_load")
        prm_load = sem("prm_load")
        t_load = [sem(f"t_load{i}") for i in range(TR)]
        k_stored = sem("k_stored")
        zeros_stored = sem("zeros_stored")
        out_stored = [sem(f"out_stored{i}") for i in range(TR)]
        consts = sem("consts")
        ident_zero = sem("ident_zero")
        w_split = sem("w_split")
        b_split = sem("b_split")
        hi_done = sem("hi_done")
        dve_own = sem("dve_own")
        masks = sem("masks")
        slot_full = sem("slot_full")
        xt_done = sem("xt_done")
        xt_hi_done = sem("xt_hi_done")
        xt_lo_done = sem("xt_lo_done")
        low_done = sem("low_done")
        low_read = sem("low_read")
        sel_done = sem("sel_done")
        lowt_done = sem("lowt_done")
        lowst_hi = sem("lowst_hi")
        lowst_hi2 = sem("lowst_hi2")
        lowst_done = sem("lowst_done")
        y_done = sem("y_done")
        y_read = sem("y_read")
        pool_own = sem("pool_own")
        k_args = sem("k_args")
        k_funcs = sem("k_funcs")
        k_den = sem("k_den")
        k_recip = sem("k_recip")
        k_factors = sem("k_factors")
        k_product = sem("k_product")
        k_out = sem("k_out")
        t_hi_done = sem("t_hi_done")
        t_lo_done = sem("t_lo_done")

        block = ctx.enter_context(nc.Block())

        def f32(ap):
            return ap.bitcast(F32)

        @block.sync
        def _(sp):
            def load_x(n):
                sp.dma_start(x_all[:, XG * n:XG * n + XG, :],
                             x[:, XG * n:XG * n + XG, :]).then_inc(x_load[n % 2], 16)

            def x_arrived(n):
                sp.wait_ge(x_load[n % 2], 16 * (n // 2 + 1))
                sp.nop().then_inc(x_here, XG)

            def load_slot(h):
                sp.dma_start(x_slot[:, h:h + 1, :], x[:, h:h + 1, :]).then_inc(slot_load[h], 16)

            def load_w(c):
                sp.dma_start(w_raw[:, c, :], wa[c * P:(c + 1) * P, :]).then_inc(w_load[c], 16)

            load_slot(0)
            load_w(0)
            load_w(1)
            load_slot(1)
            load_w(2)
            load_w(3)
            load_x(0)
            load_x(1)
            for n in range(H // XG):
                x_arrived(n)
                if n + 2 < H // XG:
                    load_x(n + 2)

            sp.wait_ge(k_out, 2)
            for j in range(HG):
                rows = k_pad[j:H:HG, 0:L].rearrange("g (a b) -> a g b", b=LB)
                sp.dma_start(rows, k_sb[LA * j:LA * j + LA, :, LB * j:LB * j + LB]).then_inc(k_stored, 16)
            sp.wait_ge(k_stored, 16 * HG)
            sp.wait_ge(zeros_stored, 16)

            def load_t(k, slot):
                window = bass.AP(k_pad.tensor, k * PADK, [[1, P], [1, L]])
                sp.dma_start(t_raw[:, slot, :], window).then_inc(t_load[slot], 16)

            def store(h, slot):
                sp.wait_ge(y_read, h + H + 1)
                sp.dma_start(out[:, bass.ds(h, 1), :], x_slot[:, slot:slot + 1, :]).then_inc(out_stored[slot], 16)

            for k in range(TR):
                load_t(k, k)
            for k in range(TR, FIRST + 4):
                sp.wait_ge(t_lo_done, k - TR + 1)
                load_t(k, k % TR)
            for h in range(FIRST):
                store(h, h)
            with sp.Fori(0, TURNS) as turn:
                for u in range(TR):
                    h = turn * TR + FIRST + u
                    sp.wait_ge(t_lo_done, h - 1)
                    load_t(h + 4, (FIRST + u + 4) % TR)
                    store(h, (FIRST + u) % TR)
            for h in range(LAST, H):
                store(h, h % TR)
            for slot in range(TR):
                sp.wait_ge(out_stored[slot], 16 * len(range(slot, H, TR)))

        @block.gpsimd
        def _(pool):
            own = [0]

            def step(ins):
                own[0] += 1
                ins.then_inc(pool_own, 1)
                pool.wait_ge(pool_own, own[0])

            g = nc.gpsimd
            g.memset(ident[:], 0.0).then_inc(ident_zero, 1)
            g.iota(lab_iota[:], pattern=[[1, NLAB], [0, RANK]], base=0, channel_multiplier=0,
                   allow_small_or_imprecise_dtypes=True).then_inc(consts, 1)
            pool.wait_ge(ident_zero, 1)
            g.affine_select(out=ident[:], in_=ident[:], compare_op=ALU.not_equal, fill=1.0, base=0,
                            pattern=[[-1, P]], channel_multiplier=1).then_inc(consts, 1)
            g.iota(l_iota[:], pattern=[[1, L]], base=0, channel_multiplier=0,
                   allow_small_or_imprecise_dtypes=True).then_inc(consts, 1)
            for half in range(2):
                rows = slice(NST * half, NST * half + NST)
                g.dma_start(logs[rows, 1, :], ssm[:, 0, :]).then_inc(prm_load, 16)
                g.dma_start(prm[rows, :, :], ssm[:, 1:4, :]).then_inc(prm_load, 16)
            g.dma_start(logs[:, 0, :], log_dt.rearrange("(o h) -> o h", o=1).broadcast_to([P, H]))\
                .then_inc(prm_load, 16)
            g.dma_start(d_row[:], d_skip.rearrange("(o h) -> o h", o=1)).then_inc(prm_load, 16)
            step(g.memset(zeros[:], 0.0))
            g.dma_start(k_pad[:, L:PADK], zeros[:]).then_inc(zeros_stored, 16)
            step(g.iota(ramp_b[:], pattern=[[-1, LB]], base=LB - 1, channel_multiplier=0,
                        allow_small_or_imprecise_dtypes=True))
            step(g.iota(ramp_a[:], pattern=[[-LB, LA]], base=LB * (LA - 1), channel_multiplier=0,
                        allow_small_or_imprecise_dtypes=True))
            step(g.memset(shift[:], 0.0))
            step(g.memset(shift[0:NST, 0:1], 0.25))
            step(g.memset(shift[NST:P, 1:2], 0.25))
            step(g.memset(sign[0:NST, :], 1.0))
            step(g.memset(sign[NST:P, :], -1.0))
            step(g.memset(k_d[:], 0.0))
            step(g.memset(k_one[:], 0.0))
            step(g.memset(k_one[:, :, LB - 1:LB], 1.0))
            pool.wait_ge(prm_load, 16 * 6)

            def ts(o, i, s1, s2, op0, op1):
                step(g.tensor_scalar(o, i, s1, s2, op0, op1))

            def tt(o, a, b, op):
                step(g.tensor_tensor(o, a, b, op))

            ts(k_d[:, :, LA - 1], d_row[:], 1.0, 1.0, ALU.add, ALU.mult)
            ts(logs[:], logs[:], -87.0, 88.0, ALU.max, ALU.min)
            ts(e_k[:], logs[:], 1.0 / math.log(2.0), ROUND, ALU.mult, ALU.add)
            ts(e_k[:], e_k[:], 1.0, -ROUND, ALU.mult, ALU.add)
            ts(e_p[:], e_k[:], -LN2_HI, 0.0, ALU.mult, ALU.add)
            tt(e_r[:], logs[:], e_p[:], ALU.add)
            ts(e_p[:], e_k[:], -LN2_LO, 0.0, ALU.mult, ALU.add)
            tt(e_r[:], e_r[:], e_p[:], ALU.add)
            ts(e_p[:], e_r[:], 1.0 / math.factorial(7), 1.0 / math.factorial(6), ALU.mult, ALU.add)
            for n in range(5, -1, -1):
                tt(e_p[:], e_p[:], e_r[:], ALU.mult)
                ts(e_p[:], e_p[:], 1.0, 1.0 / math.factorial(n), ALU.mult, ALU.add)
            ts(e_i[:], e_k[:], 127.0, float(2 ** 23), ALU.add, ALU.mult)
            tt(ex[:], e_p[:], e_i[:].bitcast(F32), ALU.mult)
            dt, neg_re = ex[:, 0, :], ex[:, 1, :]
            a_im, c_re, c_im = prm[:, 0, :], prm[:, 1, :], prm[:, 2, :]
            tt(re_dta[:], dt, neg_re, ALU.mult)
            ts(re_dta[:], re_dta[:], -1.0, 0.0, ALU.mult, ALU.add)
            ts(half_a[:], re_dta[:], 0.5, 0.0, ALU.mult, ALU.add)
            tt(turns[:], a_im, dt, ALU.mult)
            ts(turns[:], turns[:], 1.0 / (2.0 * math.pi), 0.0, ALU.mult, ALU.add)

            def outer(o, v, ramp, n):
                tt(o.rearrange("p (h n) -> p h n", n=n), v.unsqueeze(2).to_broadcast([P, H, n]),
                   ramp.unsqueeze(1).to_broadcast([P, H, n]), ALU.mult)

            q_at, u_at, v_at, s_at = 0, NQ, NQ + NP, NQ + 2 * NP
            outer(phase[:, q_at:u_at], turns[:], ramp_b[:], LB)
            outer(phase[:, u_at:v_at], turns[:], ramp_a[:], LA)
            ts(phase[:, v_at:s_at], phase[:, u_at:v_at], shift[:, 1:2], 1.0, ALU.add, ALU.mult)
            ts(phase[:, q_at:v_at], phase[:, q_at:v_at], shift[:, 0:1], 1.0, ALU.add, ALU.mult)
            ts(phase[:, s_at:s_at + H], turns[:], 0.5, 0.0, ALU.mult, ALU.add)
            ts(phase[:, s_at + H:], turns[:], 1.0, 0.0, ALU.mult, ALU.add)
            ts(whole[:], phase[:], 1.0, ROUND, ALU.mult, ALU.add)
            ts(whole[:], whole[:], 1.0, -ROUND, ALU.mult, ALU.add)
            tt(phase[:], phase[:], whole[:], ALU.subtract)
            outer(mag[:, 0:NQ], re_dta[:], ramp_b[:], LB)
            outer(mag[:, NQ:NQ + NP], re_dta[:], ramp_a[:], LA)
            g.nop().then_inc(k_args, 1)

            pool.wait_ge(k_funcs, 3)
            tanh, sin_half, sin_one = half_a[:], phase[:, s_at:s_at + H], phase[:, s_at + H:]
            q = phase[:, q_at:u_at]
            u, v = phase[:, u_at:v_at], phase[:, v_at:s_at]
            T = [tmp[:, i, :] for i in range(12)]
            tt(T[0], neg_re, neg_re, ALU.mult)
            tt(T[1], a_im, a_im, ALU.mult)
            tt(T[0], T[0], T[1], ALU.add)
            ts(T[1], tanh, -1.0, 1.0, ALU.mult, ALU.add)
            own[0] += 1
            g.tensor_tensor(T[2], T[0], T[1], ALU.mult).then_inc(pool_own, 1)
            pool.wait_ge(pool_own, own[0])
            g.nop().then_inc(k_den, 1)
            ts(T[3], tanh, 1.0, 0.0, ALU.add, ALU.add)
            tt(T[4], sin_half, sin_half, ALU.mult)
            tt(T[4], T[4], T[3], ALU.mult)
            tt(T[4], tanh, T[4], ALU.subtract)
            ts(T[4], T[4], 2.0, 0.0, ALU.mult, ALU.add)
            tt(T[5], T[3], sin_one, ALU.mult)
            tt(T[6], T[5], a_im, ALU.mult)
            tt(T[7], T[4], neg_re, ALU.mult)
            tt(T[6], T[6], T[7], ALU.subtract)
            tt(T[7], T[5], neg_re, ALU.mult)
            tt(T[8], T[4], a_im, ALU.mult)
            tt(T[7], T[7], T[8], ALU.add)
            tt(T[8], c_re, T[6], ALU.mult)
            tt(T[9], c_im, T[7], ALU.mult)
            tt(T[9], T[8], T[9], ALU.add)
            tt(T[8], c_re, T[7], ALU.mult)
            tt(T[10], c_im, T[6], ALU.mult)
            tt(T[10], T[8], T[10], ALU.subtract)
            pool.wait_ge(k_recip, 1)
            ts(recip[:], recip[:], 2.0, 0.0, ALU.mult, ALU.add)
            tt(T[9], T[9], recip[:], ALU.mult)
            ts(T[9], T[9], sign[:], 1.0, ALU.mult, ALU.mult)
            tt(T[10], T[10], recip[:], ALU.mult)
            tt(q, q, mag[:, 0:NQ], ALU.mult)
            tt(u, u, mag[:, NQ:NQ + NP], ALU.mult)
            tt(v, v, mag[:, NQ:NQ + NP], ALU.mult)

            def by_head(o, i, c):
                tt(o.rearrange("p (h n) -> p h n", n=LA), i.rearrange("p (h n) -> p h n", n=LA),
                   c.unsqueeze(2).to_broadcast([P, H, LA]), ALU.mult)

            by_head(u, u, T[9])
            by_head(v, v, T[10])
            own[0] += 1
            g.tensor_tensor(u, u, v, ALU.add).then_inc(pool_own, 1)
            pool.wait_ge(pool_own, own[0])
            g.nop().then_inc(k_factors, 1)

            def split_t(k, slot):
                pool.wait_ge(t_hi_done, k + 1)
                g.tensor_tensor(t_lo[:, slot, :], t_raw[:, slot, :], f32(t_hi[:, slot, :]),
                                ALU.subtract).then_inc(t_lo_done, 1)

            with pool.Fori(0, H // TR) as turn:
                for slot in range(TR):
                    split_t(turn * TR + slot, slot)
            for k in range(H // TR * TR, H):
                split_t(k, k % TR)

        @block.scalar
        def _(act):
            s = nc.scalar

            act.dma_start(lab_i[:], lab.rearrange("(p o) -> p o", o=1)).then_inc(idx_load, 16)
            act.dma_start(len_i[:], length.rearrange("(p o) -> p o", o=1)).then_inc(idx_load, 16)
            for r in range(3):
                act.dma_start(b_raw[r * RANK:(r + 1) * RANK, :], lora_bt).then_inc(b_load, 16)

            def fill_slot(slot, head):
                s.copy(x_slot[:, slot, :], x_all[:, head, :] if isinstance(head, int)
                       else x_all[:, bass.ds(head, 1), :]).then_inc(slot_full, 1)

            def split_xt_hi(step, slot):
                act.wait_ge(xt_done, step + 1)
                s.copy(xt_hi[:, slot, :, :], xt_ps[slot][:]).then_inc(xt_hi_done, 1)

            def split_t_hi(k, slot, turn):
                act.wait_ge(t_load[slot], 16 * (turn + 1))
                s.copy(t_hi[:, slot, :], t_raw[:, slot, :]).then_inc(t_hi_done, 1)

            def split_w_hi(c):
                act.wait_ge(w_load[c], 16)
                s.copy(w_hi[:, c, :], w_raw[:, c, :]).then_inc(hi_done, 1)

            split_xt_hi(0, 0)
            split_w_hi(0)
            split_w_hi(1)
            split_w_hi(2)
            split_w_hi(3)
            split_xt_hi(1, 1)
            act.wait_ge(b_load, 48)
            s.mul(b_stack[:], b_raw[:], LORA_SCALING).then_inc(hi_done, 1)
            act.wait_ge(x_here, 3)
            fill_slot(0, 2)

            def pass1(h, p, to_pass2=None):
                act.wait_ge(xt_done, h + 2)
                if to_pass2 is None:
                    act.wait_ge(x_here, h + 4)
                    fill_slot(1 - p, h + 3)
                else:
                    act.wait_ge(y_read, to_pass2 + 1)
                    fill_slot(to_pass2, to_pass2)
                act.wait_ge(lowt_done, h + 1)
                s.copy(low_stack[0:RANK, p, :], lowt_ps[0:RANK, 0:P]).then_inc(lowst_hi, 1)
                act.wait_ge(lowst_hi, h + 1)
                s.copy(low_stack[2 * RANK:3 * RANK, p, :], f32(low_stack[0:RANK, p, :]))\
                    .then_inc(lowst_hi2, 1)
                split_xt_hi(h + 2, p)

            def heads(first, last):
                with act.Fori(first // 2, last // 2) as pair:
                    for u in range(2):
                        pass1(pair * 2 + u, u, None)

            heads(0, ACT_KGEN_HEAD)
            act.wait_ge(k_args, 1)
            s.activation(half_a[:], half_a[:], ACT.Tanh).then_inc(k_funcs, 1)
            s.activation(mag[:], mag[:], ACT.Exp).then_inc(k_funcs, 1)
            heads(ACT_KGEN_HEAD, ACT_KGEN_HEAD + 2)
            s.activation(phase[:], phase[:], ACT.Sin, scale=2.0 * math.pi).then_inc(k_funcs, 1)
            heads(ACT_KGEN_HEAD + 2, PE_KGEN_HEAD)
            for half in range(2):
                act.wait_ge(k_product, half + 1)
                s.copy(k_sb[:, half * NG // 2:(half + 1) * NG // 2, :], k_ps[:]).then_inc(k_out, 1)
                heads(PE_KGEN_HEAD + 2 * half, PE_KGEN_HEAD + 2 * half + 2)
            heads(PE_KGEN_HEAD + 4, T_HEAD)
            for h in range(T_HEAD, H):
                pass1(h, h % 2, None if h + 3 < H else h + 3 - H)
                split_t_hi(h - T_HEAD, h - T_HEAD, 0)

            def pass2(h, u):
                act.wait_ge(y_done, h + H)
                split_xt_hi(h + H + 1, (u + 1) % 2)

            act.wait_ge(y_read, 4)
            fill_slot(3, 3)
            pass2(1, 1)
            fill_slot(4, 4)
            for h in range(2, FIRST):
                pass2(h, h)
                split_t_hi(h + 2, h + 2, 0)
                if h + 3 >= TR:
                    act.wait_ge(out_stored[(h + 3) % TR], 16)
                fill_slot((h + 3) % TR, h + 3)
            with act.Fori(0, TURNS) as turn:
                for u in range(TR):
                    h = turn * TR + FIRST + u
                    pass2(h, (FIRST + u) % TR)
                    split_t_hi(h + 2, u, turn + 1)
                    slot = (u + 1) % TR
                    act.wait_ge(out_stored[slot], (turn + 1 + (u + 1) // TR) * 16)
                    fill_slot(slot, h + 3)
            for h in range(LAST, H - 1):
                pass2(h, h % TR)
                if h + 2 < H:
                    split_t_hi(h + 2, (h + 2) % TR, (h + 2) // TR)
                if h + 3 < H:
                    act.wait_ge(out_stored[(h + 3) % TR], (h + 3) // TR * 16)
                    fill_slot((h + 3) % TR, h + 3)

        @block.tensor
        def _(pe):
            mm = nc.tensor.matmul

            def transposes(step, slot, ring):
                if not (isinstance(step, int) and step < 2):
                    pe.wait_ge(slot_full, step - 1)
                if not (isinstance(step, int) and step < 2):
                    pe.wait_ge(xt_lo_done, step - 1)
                for c in range(CH):
                    last = nc.tensor.transpose(xt_ps[slot][:, c, :], x_slot[:, ring, c * P:(c + 1) * P],
                                               ident[:])
                last.then_inc(xt_done, 1)

            def times_b(h, p):
                pe.wait_ge(lowst_hi2, h + 1)
                pe.wait_ge(lowst_done, h + 1)
                for bank in range(2):
                    last = mm(y_ps[p][:, bank, 0:HALF], low_stack[:, p, :],
                              b_stack[:, bank * HALF:(bank + 1) * HALF], start=False, stop=True,
                              skip_group_check=True)
                last.then_inc(y_done, 1)

            def pass1(h, p):
                first = isinstance(h, int) and h == 0
                pe.wait_ge(xt_hi_done, h + 1)
                pe.wait_ge(xt_lo_done, h + 1)
                if not (isinstance(h, int) and h < 2):
                    pe.wait_ge(y_read, h - 1)

                def products(bank, c, n):
                    o = y_ps[p][:, bank, 0:n]
                    w = slice(bank * HALF, bank * HALF + n)
                    mm(o, xt_hi[:, p, c, :], w_hi[:, c, w], start=(c == 0), stop=False,
                       skip_group_check=True)
                    mm(o, xt_hi[:, p, c, :], w_lo[:, c, w], start=False, stop=False,
                       skip_group_check=True)
                    return mm(o, xt_lo[:, p, c, :], w_hi[:, c, w], start=False, stop=False,
                              skip_group_check=True)

                for c in range(CH):
                    if first:
                        pe.wait_ge(w_split, c + 1)
                    last = products(1, c, WA - HALF)
                    if c == 0 and not first:
                        times_b(h - 1, 1 - p)
                last.then_inc(low_done, 1)
                for c in range(CH - 1):
                    products(0, c, HALF)
                pe.wait_ge(sel_done, h + 1)
                nc.tensor.transpose(lowt_ps[0:RANK, 0:P], low_sel[:, p, :], ident[:]).then_inc(lowt_done, 1)
                products(0, CH - 1, HALF)
                transposes(h + 2, p, p)

            def heads(first, last):
                with pe.Fori(first // 2, last // 2) as pair:
                    for u in range(2):
                        pass1(pair * 2 + u, u)

            pe.wait_ge(consts, 3)
            pe.wait_ge(slot_load[0], 16)
            transposes(0, 0, 0)
            pe.wait_ge(slot_load[1], 16)
            transposes(1, 1, 1)
            pass1(0, 0)
            pe.wait_ge(b_split, 1)
            pass1(1, 1)
            heads(2, PE_KGEN_HEAD)
            pe.wait_ge(k_factors, 1)
            for half in range(2):
                if half:
                    pe.wait_ge(k_out, half)
                for g in range(half * NG // 2, (half + 1) * NG // 2):
                    o = k_ps[:, g % (NG // 2), :]
                    pq = phase[:, NQ + g * HG * LA:NQ + (g + 1) * HG * LA]
                    mm(o, pq, phase[:, g * HG * LB:(g + 1) * HG * LB], start=True, stop=False)
                    last = mm(o, k_d[:, g * HG:(g + 1) * HG, :].rearrange("o h a -> o (h a)"),
                              k_one[:].rearrange("o h b -> o (h b)"), start=False, stop=True)
                last.then_inc(k_product, 1)
                heads(PE_KGEN_HEAD + 2 * half, PE_KGEN_HEAD + 2 * half + 2)
            heads(PE_KGEN_HEAD + 4, H - 2)
            pass1(H - 2, 0)
            pass1(H - 1, 1)

            def pass2(h, u, ahead=True, last_b=False):
                p = u % 2
                if ahead:
                    transposes(h + H + 1, 1 - p, (u + 1) % TR)
                pe.wait_ge(xt_hi_done, h + H + 1)
                pe.wait_ge(xt_lo_done, h + H + 1)
                pe.wait_ge(t_hi_done, h + 1)
                pe.wait_ge(t_lo_done, h + 1)
                pe.wait_ge(y_read, h + H - 1)
                for c in range(CH):
                    o, t = y2[p][:, 0:L - c * P], slice(c * P, L)
                    mm(o, xt_hi[:, p, c, :], t_hi[:, u, t], start=(c == 0), stop=False)
                    mm(o, xt_hi[:, p, c, :], t_lo[:, u, t], start=False, stop=False)
                    last = mm(o, xt_lo[:, p, c, :], t_hi[:, u, t], start=False, stop=(c == CH - 1))
                    if last_b and c == 0:
                        times_b(H - 1, (H - 1) % 2)
                last.then_inc(y_done, 1)

            for h in range(FIRST):
                pass2(h, h, ahead=h > 0, last_b=h == 0)
            with pe.Fori(0, TURNS) as turn:
                for u in range(TR):
                    pass2(turn * TR + FIRST + u, (FIRST + u) % TR)
            for h in range(LAST, H):
                pass2(h, h % TR, ahead=h < H - 1)

        @block.vector
        def _(dve):
            v = nc.vector
            own = [0]

            def step(ins):
                own[0] += 1
                ins.then_inc(dve_own, 1)
                dve.wait_ge(dve_own, own[0])

            def split_xt_lo(st, slot):
                dve.wait_ge(xt_hi_done, st + 1)
                v.tensor_tensor(xt_lo[:, slot, :, :], xt_ps[slot][:], f32(xt_hi[:, slot, :, :]),
                                ALU.subtract).then_inc(xt_lo_done, 1)

            dve.wait_ge(idx_load, 32)
            step(v.tensor_copy(lab_f[:], lab_i[:]))
            step(v.tensor_copy(len_f[:], len_i[:]))
            step(v.tensor_scalar(lab_neg[:], lab_f[:], 0.0, float(NLAB), ALU.is_lt, ALU.mult))
            step(v.tensor_tensor(lab_f[:], lab_f[:], lab_neg[:], ALU.add))
            step(v.tensor_scalar(lab_f[:], lab_f[:], 0.0, float(NLAB - 1), ALU.max, ALU.min))
            dve.wait_ge(consts, 3)
            v.tensor_scalar(lab_mask[:], lab_iota[:], lab_f[:], None, ALU.is_equal).then_inc(masks, 1)
            v.tensor_scalar(len_mask[:], l_iota[:], len_f[:], None, ALU.is_lt).then_inc(masks, 1)
            split_xt_lo(0, 0)
            for c in range(CH):
                dve.wait_ge(hi_done, c + 1)
                v.tensor_tensor(w_lo[:, c, :], w_raw[:, c, :], f32(w_hi[:, c, :]), ALU.subtract)\
                    .then_inc(w_split, 1)
            split_xt_lo(1, 1)
            dve.wait_ge(hi_done, CH + 1)
            lo = slice(2 * RANK, 3 * RANK)
            v.scalar_tensor_tensor(b_stack[lo, :], b_raw[lo, :], LORA_SCALING, f32(b_stack[lo, :]),
                                   ALU.mult, ALU.subtract).then_inc(b_split, 1)
            dve.wait_ge(masks, 1)

            def add_residual(h, p):
                dve.wait_ge(y_done, h + 1)
                xh = x_all[:, bass.ds(h, 1), :].rearrange("p o (b n) -> p (o b) n", b=2)
                v.tensor_tensor(xh, y1[p], xh, ALU.add).then_inc(y_read, 1)

            def pass1(h, p):
                if not (isinstance(h, int) and h == 0):
                    add_residual(h - 1, 1 - p)
                dve.wait_ge(low_done, h + 1)
                v.tensor_tensor(low_prod[:], low_ps[p], lab_mask[:].rearrange("p l r -> p (l r)"),
                                ALU.mult).then_inc(low_read, 1)
                dve.wait_ge(low_read, h + 1)
                v.tensor_reduce(low_sel[:, p, :], low_prod[:].rearrange("p (l r) -> p r l", l=NLAB),
                                AX.X, ALU.add).then_inc(sel_done, 1)
                dve.wait_ge(lowst_hi, h + 1)
                v.tensor_tensor(low_stack[RANK:2 * RANK, p, :], lowt_ps[0:RANK, 0:P],
                                f32(low_stack[0:RANK, p, :]), ALU.subtract).then_inc(lowst_done, 1)
                split_xt_lo(h + 2, p)

            def heads(first, last):
                with dve.Fori(first // 2, last // 2) as pair:
                    for u in range(2):
                        pass1(pair * 2 + u, u)

            pass1(0, 0)
            pass1(1, 1)
            heads(2, DVE_KGEN_HEAD)
            dve.wait_ge(k_den, 1)
            v.reciprocal(recip[:], tmp[:, 2, :]).then_inc(k_recip, 1)
            heads(DVE_KGEN_HEAD, H)
            add_residual(H - 1, (H - 1) % 2)

            def pass2(h, u, ahead=True):
                if ahead:
                    split_xt_lo(h + H + 1, (u + 1) % 2)
                dve.wait_ge(y_done, h + H + 1)
                v.memset(waited[:, u:u + 1], 0.0)
                dve.wait_ge(masks, 2)
                v.copy_predicated(x_slot[:, u, :], len_mask[:], y2[u % 2][:, ::-1]).then_inc(y_read, 1)

            for h in range(FIRST):
                pass2(h, h, ahead=h > 0)
            with dve.Fori(0, TURNS) as turn:
                for u in range(TR):
                    pass2(turn * TR + FIRST + u, (FIRST + u) % TR)
            for h in range(LAST, H):
                pass2(h, h % TR, ahead=h < H - 1)


def kernel(x, itok_B_0_2, itok_B_78_3631, L0_cond_W, L0_cond_lora_A, L0_cond_lora_B_w,
           L1_cond_log_dt, L1_cond_C, L1_cond_log_A_real, L1_cond_A_imag, L1_cond_D):
    import numpy as np
    import concourse.bacc as bacc
    from concourse.bass_utils import run_bass_kernel_spmd

    C = np.asarray(L1_cond_C)
    ssm = np.stack([np.asarray(L1_cond_log_A_real).T, np.asarray(L1_cond_A_imag).T,
                    C[:, :, 0].T, C[:, :, 1].T], axis=1)
    arrays = {
        "x": np.asarray(x),
        "lab": np.asarray(itok_B_0_2),
        "length": np.asarray(itok_B_78_3631),
        "wa": np.concatenate([np.asarray(L0_cond_W).T,
                              np.asarray(L0_cond_lora_A).transpose(1, 0, 2).reshape(L, LOW)], axis=1),
        "lora_bt": np.asarray(L0_cond_lora_B_w).T,
        "log_dt": np.asarray(L1_cond_log_dt),
        "ssm": ssm,
        "d_skip": np.asarray(L1_cond_D),
    }
    arrays = {"in_" + k: np.ascontiguousarray(v) for k, v in arrays.items()}
    nc = bacc.Bacc("TRN2", target_bir_lowering=False, num_devices=1)
    args = [nc.dram_tensor(k, v.shape, mybir.dt.from_np(v.dtype), kind="ExternalInput").ap()
            for k, v in arrays.items()]
    out = nc.dram_tensor("out_0", (P, H, L), F32, kind="ExternalOutput").ap()
    conditioned_residual(nc, *args, out)
    r = run_bass_kernel_spmd(nc, [arrays], core_ids=[0])
    return r.results[0]["out_0"]
```

```python
from contextlib import ExitStack
import math

import concourse.bass as bass
from concourse import mybir

F32 = mybir.dt.float32
F32R = mybir.dt.float32r
BF16 = mybir.dt.bfloat16
I32 = mybir.dt.int32
ALU = mybir.AluOpType
ACT = mybir.ActivationFunctionType
AX = mybir.AxisListType

P = 128
H = 32
L = 512
CH = L // P
NLAB = 5
RANK = 32
LOW = NLAB * RANK
LORA_SCALING = 0.5
NST = 64
LB = 32
LA = L // LB
HG = P // LA
NG = H // HG
PADK = P + L
TR = 6
FIRST, TURNS = 4, 4
LAST = FIRST + TURNS * TR
HALF = L // 2
WA = L + LOW
WARM = 10
XG = 4
PIECES = [(0, slice(HALF, WA)), (0, slice(0, HALF)), (1, slice(HALF, WA)), (1, slice(0, HALF)),
          (2, slice(0, WA)), (3, slice(0, WA))]
UNROLL = 4

ACT_KGEN_HEAD = 12
DVE_KGEN_HEAD = 16
PE_KGEN_HEAD = 24
PE_UNROLL = (PE_KGEN_HEAD - UNROLL) // 2
T_HEAD = H - 4

ROUND = 1.5 * 2.0 ** 23
LN2_HI = 0.693145751953125
LN2_LO = 1.42860682030941723e-6


def conditioned_residual(nc, xt, idx, wa, lora_bt, log_dt, ssm, d_skip, out):
    ctx = ExitStack()
    with ctx:
        def sb(name, shape, dt=F32):
            return ctx.enter_context(nc.sbuf_tensor(name, shape, dt))

        def ps(name, shape):
            return ctx.enter_context(nc.psum_tensor(name, shape, F32))

        def sem(name):
            return ctx.enter_context(nc.semaphore(name))

        x_all = sb("x_all", [P, H, L])
        x_slot = sb("x_slot", [P, TR, L])
        xt_hi = sb("xt_hi", [P, 2, L], F32R)
        xt_lo = sb("xt_lo", [P, 2, L], F32R)
        w_raw = sb("w_raw", [P, CH, WA])
        w_hi = sb("w_hi", [P, CH, WA], F32R)
        w_lo = sb("w_lo", [P, CH, WA], F32R)
        b_raw = sb("b_raw", [3 * RANK, L])
        b_stack = sb("b_stack", [3 * RANK, L], F32R)
        low_stack = sb("low_stack", [3 * RANK, 2, P], F32R)
        wait_mark = sb("wait_mark", [1, TR])
        low_prod = sb("low_prod", [P, 2, LOW])
        low_sel = sb("low_sel", [P, 2, RANK])
        warm = sb("warm", [P, L], BF16)
        ident = sb("ident", [P, P])
        idx_i = sb("idx_i", [P, 2], I32)
        idx_f = sb("idx_f", [P, 2])
        lab_neg = sb("lab_neg", [P, 1])
        lab_iota = sb("lab_iota", [P, NLAB, RANK])
        lab_mask = sb("lab_mask", [P, NLAB, RANK])
        l_iota = sb("l_iota", [P, L])
        len_mask = sb("len_mask", [P, L], I32)
        logs = sb("logs", [P, 2, H])
        prm = sb("prm", [P, 3, H])
        d_row = sb("d_row", [1, H])
        ex = sb("ex", [P, 2, H])
        e_k = sb("e_k", [P, 2, H])
        e_r = sb("e_r", [P, 2, H])
        e_p = sb("e_p", [P, 2, H])
        e_i = sb("e_i", [P, 2, H], I32)
        half_a = sb("half_a", [P, H])
        re_dta = sb("re_dta", [P, H])
        turns = sb("turns", [P, H])
        tmp = sb("tmp", [P, 12, H])
        recip = sb("recip", [P, H])
        ramp_b = sb("ramp_b", [P, LB])
        ramp_a = sb("ramp_a", [P, LA])
        shift = sb("shift", [P, 2])
        sign = sb("sign", [P, 1])
        NQ, NP = H * LB, H * LA
        phase = sb("phase", [P, NQ + 2 * NP + 2 * H])
        whole = sb("whole", [P, NQ + 2 * NP + 2 * H])
        mag = sb("mag", [P, NQ + NP])
        k_d = sb("k_d", [1, H, LA])
        k_one = sb("k_one", [1, HG])
        k_sb = sb("k_sb", [P, NG, HG * LB])
        zeros = sb("zeros", [H, P])
        t_raw = sb("t_raw", [P, TR, L])
        t_hi = sb("t_hi", [P, TR, L], F32R)
        t_lo = sb("t_lo", [P, TR, L], F32R)
        k_pad = nc.dram_tensor("k_pad", (H, PADK), F32).ap()

        turn_ps = ps("turn_ps", [P, 2, L])
        y_ps = [ps(f"y_ps{i}", [P, 2, L]) for i in range(2)] + [turn_ps]
        lowt_ps = ps("lowt_ps", [P, 2, L])
        xt_ps = [turn_ps[:, i, :] for i in range(2)]
        k_ps = turn_ps[:].rearrange("p b (g n) -> p (b g) n", n=HG * LB)
        y1 = [y[:, :, 0:HALF] for y in y_ps]
        low_ps = [y[:, 1, HALF:HALF + LOW] for y in y_ps]
        y2 = [y[:, 0, :] for y in y_ps]
        x_hi = [xt_hi[:, 0, :], xt_hi[:, 1, :], t_hi[:, 0, :], t_hi[:, 1, :]]
        x_lo = [xt_lo[:, 0, :], xt_lo[:, 1, :], t_lo[:, 0, :], t_lo[:, 1, :]]

        x_load = [sem(f"x_load{i}") for i in range(3)]
        x_here = sem("x_here")
        w_load = [sem(f"w_load{c}") for c in range(CH)]
        w_load_first = sem("w_load_first")
        b_load = sem("b_load")
        idx_load = sem("idx_load")
        prm_load = sem("prm_load")
        t_load = [sem(f"t_load{i}") for i in range(TR)]
        k_stored = sem("k_stored")
        zeros_stored = sem("zeros_stored")
        out_stored = [sem(f"out_stored{i}") for i in range(TR)]
        warm_zero = sem("warm_zero")
        consts = sem("consts")
        ident_zero = sem("ident_zero")
        w_plus_dve = sem("w_plus_dve")
        w_plus = sem("w_plus")
        w_split = sem("w_split")
        b_split = sem("b_split")
        hi_done = sem("hi_done")
        dve_own = sem("dve_own")
        masks = sem("masks")
        x_used = sem("x_used")
        slot_full = sem("slot_full")
        xt_done = sem("xt_done")
        xt_hi_done = sem("xt_hi_done")
        xt_lo_done = sem("xt_lo_done")
        low_done = sem("low_done")
        low_read = sem("low_read")
        sel_done = sem("sel_done")
        lowt_done = sem("lowt_done")
        lowst_hi = sem("lowst_hi")
        lowst_hi2 = sem("lowst_hi2")
        lowst_done = sem("lowst_done")
        y_done = sem("y_done")
        y_read = sem("y_read")
        pool_own = sem("pool_own")
        k_args = sem("k_args")
        k_funcs = sem("k_funcs")
        k_den = sem("k_den")
        k_recip = sem("k_recip")
        k_factors = sem("k_factors")
        k_product = sem("k_product")
        k_out = sem("k_out")
        t_hi_done = sem("t_hi_done")
        t_lo_done = sem("t_lo_done")

        block = ctx.enter_context(nc.Block())

        def f32(ap):
            return ap.bitcast(F32)

        @block.sync
        def _(sp):
            def load_x(first, last, i):
                sp.dma_start(x_all[:, first:last, :], xt[:, first:last, :]).then_inc(x_load[i % 3], 16)

            def x_arrived(first, last, i):
                sp.wait_ge(x_load[i % 3], 16 * (i // 3 + 1))
                sp.nop().then_inc(x_here, last - first)

            def load_w(c):
                w = slice(0, HALF if c == 0 else WA)
                sp.dma_start(w_raw[:, c, w], wa[c * P:(c + 1) * P, w]).then_inc(w_load[c], 16)

            loads = [(0, 1), (1, 2), (2, XG)] + [(h, h + XG) for h in range(XG, H, XG)]
            load_x(*loads[0], 0)
            c, w = PIECES[0]
            sp.dma_start(w_raw[:, c, w], wa[0:P, w]).then_inc(w_load_first, 16)
            load_w(0)
            load_x(*loads[1], 1)
            load_w(1)
            load_w(2)
            load_w(3)
            sp.dma_start(idx_i[:], idx).then_inc(idx_load, 16)
            load_x(*loads[2], 2)
            for r in range(3):
                sp.dma_start(b_raw[r * RANK:(r + 1) * RANK, :], lora_bt).then_inc(b_load, 16)
            for half in range(2):
                rows = slice(NST * half, NST * half + NST)
                sp.dma_start(logs[rows, 1, :], ssm[:, 0, :]).then_inc(prm_load, 16)
                sp.dma_start(prm[rows, :, :], ssm[:, 1:4, :]).then_inc(prm_load, 16)
            sp.dma_start(logs[:, 0, :], log_dt.rearrange("(o h) -> o h", o=1).broadcast_to([P, H]))\
                .then_inc(prm_load, 16)
            sp.dma_start(d_row[:], d_skip.rearrange("(o h) -> o h", o=1)).then_inc(prm_load, 16)
            for i, (first, last) in enumerate(loads):
                x_arrived(first, last, i)
                if i + 3 < len(loads):
                    load_x(*loads[i + 3], i + 3)
            sp.wait_ge(consts, 4)
            sp.dma_start(k_pad[:, L:PADK], zeros[:]).then_inc(zeros_stored, 16)

            sp.wait_ge(k_out, 1)
            for j in range(HG):
                rows = k_pad[j:H:HG, 0:L].rearrange("g (a b) -> a g b", b=LB)
                sp.dma_start(rows, k_sb[LA * j:LA * j + LA, :, LB * j:LB * j + LB]).then_inc(k_stored, 16)
            sp.wait_ge(k_stored, 16 * HG)
            sp.wait_ge(zeros_stored, 16)

            def load_t(k, slot):
                window = bass.AP(k_pad.tensor, k * PADK, [[1, P], [1, L]])
                sp.dma_start(t_raw[:, slot, :], window).then_inc(t_load[slot], 16)

            def store(h, slot):
                sp.wait_ge(y_read, h + H + 1)
                sp.dma_start(out[:, bass.ds(h, 1), :], x_slot[:, slot:slot + 1, :]).then_inc(out_stored[slot], 16)

            for k in range(TR):
                load_t(k, k)
            for k in range(TR, FIRST + 4):
                sp.wait_ge(t_lo_done, k - TR + 1)
                load_t(k, k % TR)
            for h in range(FIRST):
                store(h, h)
            with sp.Fori(0, TURNS) as turn:
                for u in range(TR):
                    h = turn * TR + FIRST + u
                    sp.wait_ge(t_lo_done, h - 1)
                    load_t(h + 4, (FIRST + u + 4) % TR)
                    store(h, (FIRST + u) % TR)
            for h in range(LAST, H - 1):
                store(h, h % TR)
            u = (H - 1) % TR
            for half in range(2):
                cols = slice(half * HALF, (half + 1) * HALF)
                sp.wait_ge(y_read, 2 * H + half)
                sp.dma_start(out[:, H - 1:H, cols], x_slot[:, u:u + 1, cols]).then_inc(out_stored[u], 16)
            for slot in range(TR):
                sp.wait_ge(out_stored[slot], 16 * (len(range(slot, H, TR)) + (slot == u)))

        @block.gpsimd
        def _(pool):
            own = [0]

            def step(ins):
                own[0] += 1
                ins.then_inc(pool_own, 1)
                pool.wait_ge(pool_own, own[0])

            g = nc.gpsimd
            g.memset(ident[:], 0.0).then_inc(ident_zero, 1)
            pool.wait_ge(ident_zero, 1)
            g.affine_select(out=ident[:], in_=ident[:], compare_op=ALU.not_equal, fill=1.0, base=0,
                            pattern=[[-1, P]], channel_multiplier=1).then_inc(consts, 1)
            g.iota(lab_iota[:], pattern=[[1, NLAB], [0, RANK]], base=0, channel_multiplier=0,
                   allow_small_or_imprecise_dtypes=True).then_inc(consts, 1)
            g.iota(l_iota[:], pattern=[[1, L]], base=0, channel_multiplier=0,
                   allow_small_or_imprecise_dtypes=True).then_inc(consts, 1)
            g.memset(zeros[:], 0.0).then_inc(consts, 1)
            step(g.iota(ramp_b[:], pattern=[[-1, LB]], base=LB - 1, channel_multiplier=0,
                        allow_small_or_imprecise_dtypes=True))
            step(g.iota(ramp_a[:], pattern=[[-LB, LA]], base=LB * (LA - 1), channel_multiplier=0,
                        allow_small_or_imprecise_dtypes=True))
            step(g.memset(shift[:], 0.0))
            step(g.memset(shift[0:NST, 0:1], 0.25))
            step(g.memset(shift[NST:P, 1:2], 0.25))
            step(g.memset(sign[0:NST, :], 1.0))
            step(g.memset(sign[NST:P, :], -1.0))
            step(g.memset(k_d[:], 0.0))
            step(g.memset(k_one[:], 1.0))
            for c in range(1, CH):
                d = slice(c * P, c * P + P)
                pool.wait_ge(w_load[c], 16)
                g.tensor_tensor(w_raw[:, c, d], w_raw[:, c, d], ident[:], ALU.add).then_inc(w_plus, 1)
            pool.wait_ge(prm_load, 16 * 6)

            def ts(o, i, s1, s2, op0, op1):
                step(g.tensor_scalar(o, i, s1, s2, op0, op1))

            def tt(o, a, b, op):
                step(g.tensor_tensor(o, a, b, op))

            ts(k_d[:, :, LA - 1], d_row[:], 1.0, 1.0, ALU.add, ALU.mult)
            ts(logs[:], logs[:], -87.0, 88.0, ALU.max, ALU.min)
            ts(e_k[:], logs[:], 1.0 / math.log(2.0), ROUND, ALU.mult, ALU.add)
            ts(e_k[:], e_k[:], 1.0, -ROUND, ALU.mult, ALU.add)
            ts(e_p[:], e_k[:], -LN2_HI, 0.0, ALU.mult, ALU.add)
            tt(e_r[:], logs[:], e_p[:], ALU.add)
            ts(e_p[:], e_k[:], -LN2_LO, 0.0, ALU.mult, ALU.add)
            tt(e_r[:], e_r[:], e_p[:], ALU.add)
            ts(e_p[:], e_r[:], 1.0 / math.factorial(7), 1.0 / math.factorial(6), ALU.mult, ALU.add)
            for n in range(5, -1, -1):
                tt(e_p[:], e_p[:], e_r[:], ALU.mult)
                ts(e_p[:], e_p[:], 1.0, 1.0 / math.factorial(n), ALU.mult, ALU.add)
            ts(e_i[:], e_k[:], 127.0, float(2 ** 23), ALU.add, ALU.mult)
            tt(ex[:], e_p[:], e_i[:].bitcast(F32), ALU.mult)
            dt, neg_re = ex[:, 0, :], ex[:, 1, :]
            a_im, c_re, c_im = prm[:, 0, :], prm[:, 1, :], prm[:, 2, :]
            tt(re_dta[:], dt, neg_re, ALU.mult)
            ts(re_dta[:], re_dta[:], -1.0, 0.0, ALU.mult, ALU.add)
            ts(half_a[:], re_dta[:], 0.5, 0.0, ALU.mult, ALU.add)
            tt(turns[:], a_im, dt, ALU.mult)
            ts(turns[:], turns[:], 1.0 / (2.0 * math.pi), 0.0, ALU.mult, ALU.add)

            def outer(o, v, ramp, n):
                tt(o.rearrange("p (h n) -> p h n", n=n), v.unsqueeze(2).to_broadcast([P, H, n]),
                   ramp.unsqueeze(1).to_broadcast([P, H, n]), ALU.mult)

            q_at, u_at, v_at, s_at = 0, NQ, NQ + NP, NQ + 2 * NP
            outer(phase[:, q_at:u_at], turns[:], ramp_b[:], LB)
            outer(phase[:, u_at:v_at], turns[:], ramp_a[:], LA)
            ts(phase[:, v_at:s_at], phase[:, u_at:v_at], shift[:, 1:2], 1.0, ALU.add, ALU.mult)
            ts(phase[:, q_at:v_at], phase[:, q_at:v_at], shift[:, 0:1], 1.0, ALU.add, ALU.mult)
            ts(phase[:, s_at:s_at + H], turns[:], 0.5, 0.0, ALU.mult, ALU.add)
            ts(phase[:, s_at + H:], turns[:], 1.0, 0.0, ALU.mult, ALU.add)
            ts(whole[:], phase[:], 1.0, ROUND, ALU.mult, ALU.add)
            ts(whole[:], whole[:], 1.0, -ROUND, ALU.mult, ALU.add)
            tt(phase[:], phase[:], whole[:], ALU.subtract)
            outer(mag[:, 0:NQ], re_dta[:], ramp_b[:], LB)
            outer(mag[:, NQ:NQ + NP], re_dta[:], ramp_a[:], LA)
            g.nop().then_inc(k_args, 1)

            pool.wait_ge(k_funcs, 3)
            tanh, sin_half, sin_one = half_a[:], phase[:, s_at:s_at + H], phase[:, s_at + H:]
            q = phase[:, q_at:u_at]
            u, v = phase[:, u_at:v_at], phase[:, v_at:s_at]
            T = [tmp[:, i, :] for i in range(12)]
            tt(T[0], neg_re, neg_re, ALU.mult)
            tt(T[1], a_im, a_im, ALU.mult)
            tt(T[0], T[0], T[1], ALU.add)
            ts(T[1], tanh, -1.0, 1.0, ALU.mult, ALU.add)
            own[0] += 1
            g.tensor_tensor(T[2], T[0], T[1], ALU.mult).then_inc(pool_own, 1)
            pool.wait_ge(pool_own, own[0])
            g.nop().then_inc(k_den, 1)
            ts(T[3], tanh, 1.0, 0.0, ALU.add, ALU.add)
            tt(T[4], sin_half, sin_half, ALU.mult)
            tt(T[4], T[4], T[3], ALU.mult)
            tt(T[4], tanh, T[4], ALU.subtract)
            ts(T[4], T[4], 2.0, 0.0, ALU.mult, ALU.add)
            tt(T[5], T[3], sin_one, ALU.mult)
            tt(T[6], T[5], a_im, ALU.mult)
            tt(T[7], T[4], neg_re, ALU.mult)
            tt(T[6], T[6], T[7], ALU.subtract)
            tt(T[7], T[5], neg_re, ALU.mult)
            tt(T[8], T[4], a_im, ALU.mult)
            tt(T[7], T[7], T[8], ALU.add)
            tt(T[8], c_re, T[6], ALU.mult)
            tt(T[9], c_im, T[7], ALU.mult)
            tt(T[9], T[8], T[9], ALU.add)
            tt(T[8], c_re, T[7], ALU.mult)
            tt(T[10], c_im, T[6], ALU.mult)
            tt(T[10], T[8], T[10], ALU.subtract)
            pool.wait_ge(k_recip, 1)
            ts(recip[:], recip[:], 2.0, 0.0, ALU.mult, ALU.add)
            tt(T[9], T[9], recip[:], ALU.mult)
            ts(T[9], T[9], sign[:], 1.0, ALU.mult, ALU.mult)
            tt(T[10], T[10], recip[:], ALU.mult)
            tt(q, q, mag[:, 0:NQ], ALU.mult)
            tt(u, u, mag[:, NQ:NQ + NP], ALU.mult)
            tt(v, v, mag[:, NQ:NQ + NP], ALU.mult)

            def by_head(o, i, c):
                tt(o.rearrange("p (h n) -> p h n", n=LA), i.rearrange("p (h n) -> p h n", n=LA),
                   c.unsqueeze(2).to_broadcast([P, H, LA]), ALU.mult)

            by_head(u, u, T[9])
            by_head(v, v, T[10])
            own[0] += 1
            g.tensor_tensor(u, u, v, ALU.add).then_inc(pool_own, 1)
            pool.wait_ge(pool_own, own[0])
            g.nop().then_inc(k_factors, 1)

            def split_t(k, slot):
                pool.wait_ge(t_hi_done, k + 1)
                g.tensor_tensor(t_lo[:, slot, :], t_raw[:, slot, :], f32(t_hi[:, slot, :]),
                                ALU.subtract).then_inc(t_lo_done, 1)

            with pool.Fori(0, H // TR) as turn:
                for slot in range(TR):
                    split_t(turn * TR + slot, slot)
            for k in range(H // TR * TR, H):
                split_t(k, k % TR)

        @block.scalar
        def _(act):
            s = nc.scalar

            def fill_slot(slot, head):
                s.copy(x_slot[:, slot, :], x_all[:, bass.ds(head, 1), :]).then_inc(slot_full, 1)

            def split_x_hi(h, slot):
                if isinstance(h, int) and h < 4:
                    act.wait_ge(x_load[min(h, 2)], 16)
                else:
                    act.wait_ge(x_here, h + 1)
                    act.wait_ge(x_used, h - 1)
                s.copy(x_hi[slot], x_all[:, bass.ds(h, 1), :]).then_inc(xt_hi_done, 1)

            def split_x1_hi(h, slot):
                act.wait_ge(xt_done, h + 1)
                s.copy(x_hi[slot], xt_ps[slot]).then_inc(xt_hi_done, 1)

            def split_t_hi(k, slot, turn):
                act.wait_ge(t_load[slot], 16 * (turn + 1))
                s.copy(t_hi[:, slot, :], t_raw[:, slot, :]).then_inc(t_hi_done, 1)

            split_x_hi(0, 0)
            for i, (c, w) in enumerate(PIECES):
                if i == 0:
                    act.wait_ge(w_load_first, 16)
                elif i == 1:
                    act.wait_ge(w_plus_dve, 1)
                elif i == 2:
                    act.wait_ge(w_load[c], 16)
                else:
                    act.wait_ge(w_plus, c)
                s.copy(w_hi[:, c, w], w_raw[:, c, w]).then_inc(hi_done, 1)
                if i == 1:
                    split_x_hi(1, 1)
            split_x_hi(2, 2)
            split_x_hi(3, 3)
            act.wait_ge(b_load, 48)
            s.mul(b_stack[:], b_raw[:], LORA_SCALING).then_inc(hi_done, 1)

            def turned_low(h, p):
                act.wait_ge(lowt_done, h + 1)
                s.copy(low_stack[0:RANK, p, :], lowt_ps[0:RANK, p, 0:P]).then_inc(lowst_hi, 1)
                act.wait_ge(lowst_hi, h + 1)
                s.copy(low_stack[2 * RANK:3 * RANK, p, :], f32(low_stack[0:RANK, p, :]))\
                    .then_inc(lowst_hi2, 1)

            def pass1(h, p, last=False):
                turned_low(h, p)
                if last:
                    split_x1_hi(h + 2 - H, p)
                else:
                    split_x_hi(h + 2, p)

            def heads(first, last):
                with act.Fori(0, (last - first) // UNROLL) as turn:
                    for u in range(UNROLL):
                        pass1(turn * UNROLL + first + u, (first + u) % 2)

            turned_low(0, 0)
            turned_low(1, 1)
            turned_low(2, 0)
            split_x_hi(4, 0)
            pass1(3, 1)
            heads(UNROLL, ACT_KGEN_HEAD)
            act.wait_ge(k_args, 1)
            s.activation(half_a[:], half_a[:], ACT.Tanh).then_inc(k_funcs, 1)
            s.activation(mag[:], mag[:], ACT.Exp).then_inc(k_funcs, 1)
            pass1(ACT_KGEN_HEAD, 0)
            pass1(ACT_KGEN_HEAD + 1, 1)
            s.activation(phase[:], phase[:], ACT.Sin, scale=2.0 * math.pi).then_inc(k_funcs, 1)
            pass1(ACT_KGEN_HEAD + 2, 0)
            pass1(ACT_KGEN_HEAD + 3, 1)
            heads(ACT_KGEN_HEAD + UNROLL, PE_KGEN_HEAD)
            act.wait_ge(k_product, 1)
            s.copy(k_sb[:], k_ps).then_inc(k_out, 1)
            for h in range(PE_KGEN_HEAD, T_HEAD):
                pass1(h, h % 2)
            for h in range(T_HEAD, H):
                if h > T_HEAD:
                    k = h - T_HEAD - 1
                    act.wait_ge(y_read, k + 1)
                    fill_slot(k, k)
                pass1(h, h % 2, last=h + 2 >= H)
                split_t_hi(h - T_HEAD, h - T_HEAD, 0)

            def pass2(h, u):
                act.wait_ge(y_done, h + H)
                split_x1_hi(h + 1, (u + 1) % 2)

            act.wait_ge(y_read, 4)
            fill_slot(3, 3)
            pass2(1, 1)
            fill_slot(4, 4)
            for h in range(2, FIRST):
                pass2(h, h)
                split_t_hi(h + 2, h + 2, 0)
                if h + 3 >= TR:
                    act.wait_ge(out_stored[(h + 3) % TR], 16)
                fill_slot((h + 3) % TR, h + 3)
            with act.Fori(0, TURNS) as turn:
                for u in range(TR):
                    h = turn * TR + FIRST + u
                    pass2(h, (FIRST + u) % TR)
                    split_t_hi(h + 2, u, turn + 1)
                    slot = (u + 1) % TR
                    act.wait_ge(out_stored[slot], (turn + 1 + (u + 1) // TR) * 16)
                    fill_slot(slot, h + 3)
            for h in range(LAST, H - 1):
                pass2(h, h % TR)
                if h + 2 < H:
                    split_t_hi(h + 2, (h + 2) % TR, (h + 2) // TR)
                if h + 3 < H:
                    act.wait_ge(out_stored[(h + 3) % TR], (h + 3) // TR * 16)
                    fill_slot((h + 3) % TR, h + 3)

        @block.tensor
        def _(pe):
            mm = nc.tensor.matmul

            def transposes(h, slot, ring):
                pe.wait_ge(slot_full, h + 1)
                if not (isinstance(h, int) and h < 2):
                    pe.wait_ge(xt_lo_done, h + H - 1)
                for c in range(CH):
                    xc = slice(c * P, (c + 1) * P)
                    last = nc.tensor.transpose(xt_ps[slot][:, xc], x_slot[:, ring, xc], ident[:])
                last.then_inc(xt_done, 1)

            def times_b(h, p, y):
                pe.wait_ge(lowst_hi2, h + 1)
                pe.wait_ge(lowst_done, h + 1)
                for bank in range(2):
                    last = mm(y_ps[y][:, bank, 0:HALF], low_stack[:, p, :],
                              b_stack[:, bank * HALF:(bank + 1) * HALF], start=False, stop=True,
                              skip_group_check=True)
                last.then_inc(y_done, 1)

            def products(p, y, bank, c):
                n = HALF if bank == 0 else WA - HALF
                o = y_ps[y][:, bank, 0:n]
                w = slice(bank * HALF, bank * HALF + n)
                hi, lo = (t[p][:, c * P:(c + 1) * P] for t in (x_hi, x_lo))
                mm(o, hi, w_hi[:, c, w], start=(c == 0), stop=False, skip_group_check=True)
                mm(o, hi, w_lo[:, c, w], start=False, stop=False, skip_group_check=True)
                return mm(o, lo, w_hi[:, c, w], start=False, stop=False, skip_group_check=True)

            def turn_low(h, p):
                pe.wait_ge(sel_done, h + 1)
                nc.tensor.transpose(lowt_ps[0:RANK, p, 0:P], low_sel[:, p, :], ident[:]).then_inc(lowt_done, 1)

            def wait_x(h):
                pe.wait_ge(xt_hi_done, h + 1)
                pe.wait_ge(xt_lo_done, h + 1)

            def pass1(h, p, slot=None, read=None, last_y=None, to_pass2=False):
                slot = p if slot is None else slot
                wait_x(h)
                pe.wait_ge(y_read, h - 1 if read is None else read)
                for c in range(CH):
                    last = products(slot, p, 1, c)
                    if c == 1:
                        times_b(h - 1, 1 - p, 1 - p if last_y is None else last_y)
                last.then_inc(low_done, 1)
                for c in range(CH - 1):
                    products(slot, p, 0, c)
                turn_low(h, p)
                products(slot, p, 0, CH - 1).then_inc(x_used, 1)
                if to_pass2:
                    transposes(h + 2 - H, p, h + 2 - H)

            def heads(first, last):
                with pe.Fori(0, (last - first) // PE_UNROLL) as turn:
                    for u in range(PE_UNROLL):
                        pass1(turn * PE_UNROLL + first + u, (first + u) % 2)

            pe.wait_ge(warm_zero, 1)
            for _ in range(WARM):
                mm(lowt_ps[:, 1, :], warm[:, 0:P], warm[:], start=True, stop=True)

            y_of = (1, 0, 2)
            piece_of = ((2, 1), (4, 3), (5, 5), (6, 6))
            for h, c in ((0, 0), (1, 0), (0, 1), (1, 1), (0, 2), (1, 2), (2, 0), (2, 1), (2, 2)):
                if c == 0:
                    wait_x(h)
                pe.wait_ge(w_split, piece_of[c][1])
                products(h, y_of[h], 1, c)
                pe.wait_ge(w_split, piece_of[c][0])
                products(h, y_of[h], 0, c)
            pe.wait_ge(w_split, len(PIECES))
            for h in range(3):
                products(h, y_of[h], 1, CH - 1).then_inc(low_done, 1)
            turn_low(0, 0)
            products(0, y_of[0], 0, CH - 1).then_inc(x_used, 1)
            turn_low(1, 1)
            products(1, y_of[1], 0, CH - 1).then_inc(x_used, 1)
            pe.wait_ge(b_split, 1)
            times_b(0, 0, y_of[0])
            products(2, y_of[2], 0, CH - 1).then_inc(x_used, 1)
            times_b(1, 1, y_of[1])
            turn_low(2, 0)
            pass1(3, 1, slot=3, read=1, last_y=y_of[2])
            heads(UNROLL, PE_KGEN_HEAD)
            pe.wait_ge(k_factors, 1)
            for g in range(NG):
                pq = phase[:, NQ + g * HG * LA:NQ + (g + 1) * HG * LA]
                mm(k_ps[:, g, :], pq, phase[:, g * HG * LB:(g + 1) * HG * LB], start=True, stop=False,
                   skip_group_check=True)
                at_zero = k_ps[:, g, :].rearrange("p (h b) -> p h b", b=LB)[:, :, LB - 1]
                last = mm(at_zero, k_d[:, g * HG:(g + 1) * HG, :].rearrange("o h a -> o (h a)"),
                          k_one[:], start=False, stop=True, skip_group_check=True)
            last.then_inc(k_product, 1)
            for h in range(PE_KGEN_HEAD, T_HEAD):
                pass1(h, h % 2)
            for h in range(T_HEAD, H):
                if h == H - 2:
                    pe.wait_ge(k_out, 1)
                pass1(h, h % 2, to_pass2=h + 2 >= H)

            def pass2(h, u, ahead=True, last_b=False):
                p = u % 2
                if ahead:
                    transposes(h + 1, 1 - p, (u + 1) % TR)
                pe.wait_ge(xt_hi_done, h + H + 1)
                pe.wait_ge(xt_lo_done, h + H + 1)
                pe.wait_ge(t_hi_done, h + 1)
                pe.wait_ge(t_lo_done, h + 1)
                pe.wait_ge(y_read, h + H - 1)
                for c in range(CH):
                    o, t, xc = y2[p][:, 0:L - c * P], slice(c * P, L), slice(c * P, (c + 1) * P)
                    mm(o, xt_hi[:, p, xc], t_hi[:, u, t], start=(c == 0), stop=False)
                    mm(o, xt_hi[:, p, xc], t_lo[:, u, t], start=False, stop=False)
                    last = mm(o, xt_lo[:, p, xc], t_hi[:, u, t], start=False, stop=(c == CH - 1))
                    if last_b and c == 0:
                        times_b(H - 1, 1, 1)
                last.then_inc(y_done, 1)

            for h in range(FIRST):
                pass2(h, h, ahead=h > 0, last_b=h == 0)
            with pe.Fori(0, TURNS) as turn:
                for u in range(TR):
                    pass2(turn * TR + FIRST + u, (FIRST + u) % TR)
            for h in range(LAST, H - 1):
                pass2(h, h % TR)
            u, p = (H - 1) % TR, (H - 1) % 2
            pe.wait_ge(xt_hi_done, 2 * H)
            pe.wait_ge(xt_lo_done, 2 * H)
            pe.wait_ge(t_hi_done, H)
            pe.wait_ge(t_lo_done, H)
            pe.wait_ge(y_read, 2 * H - 2)
            for half in range(2):
                chunks = (half + 1) * CH // 2
                for c in range(chunks):
                    m0 = (1 - half) * HALF
                    n = min(HALF, L - c * P - m0)
                    o, t = y_ps[p][:, half, 0:n], slice(c * P + m0, c * P + m0 + n)
                    xc = slice(c * P, (c + 1) * P)
                    mm(o, xt_hi[:, p, xc], t_hi[:, u, t], start=(c == 0), stop=False)
                    mm(o, xt_hi[:, p, xc], t_lo[:, u, t], start=False, stop=False)
                    last = mm(o, xt_lo[:, p, xc], t_hi[:, u, t], start=False, stop=(c == chunks - 1))
                last.then_inc(y_done, 1)

        @block.vector
        def _(dve):
            v = nc.vector
            own = [0]

            def step(ins):
                own[0] += 1
                ins.then_inc(dve_own, 1)
                dve.wait_ge(dve_own, own[0])

            def split_x_lo(h, slot):
                dve.wait_ge(xt_hi_done, h + 1)
                v.tensor_tensor(x_lo[slot], x_all[:, bass.ds(h, 1), :], f32(x_hi[slot]),
                                ALU.subtract).then_inc(xt_lo_done, 1)

            def split_x1_lo(h, slot):
                dve.wait_ge(xt_hi_done, h + H + 1)
                v.tensor_tensor(x_lo[slot], xt_ps[slot], f32(x_hi[slot]), ALU.subtract)\
                    .then_inc(xt_lo_done, 1)

            v.memset(warm[:], 0.0).then_inc(warm_zero, 1)
            split_x_lo(0, 0)
            dve.wait_ge(consts, 1)
            dve.wait_ge(w_load[0], 16)
            v.tensor_tensor(w_raw[:, 0, 0:P], w_raw[:, 0, 0:P], ident[:], ALU.add).then_inc(w_plus_dve, 1)
            for i, (c, w) in enumerate(PIECES):
                dve.wait_ge(hi_done, i + 1)
                v.tensor_tensor(w_lo[:, c, w], w_raw[:, c, w], f32(w_hi[:, c, w]), ALU.subtract)\
                    .then_inc(w_split, 1)
                if i == 1:
                    split_x_lo(1, 1)
            split_x_lo(2, 2)
            dve.wait_ge(idx_load, 16)
            lab_f, len_f = idx_f[:, 0:1], idx_f[:, 1:2]
            step(v.tensor_copy(idx_f[:], idx_i[:]))
            step(v.tensor_scalar(lab_neg[:], lab_f, 0.0, float(NLAB), ALU.is_lt, ALU.mult))
            step(v.tensor_tensor(lab_f, lab_f, lab_neg[:], ALU.add))
            step(v.tensor_scalar(lab_f, lab_f, 0.0, float(NLAB - 1), ALU.max, ALU.min))
            dve.wait_ge(consts, 3)
            v.tensor_scalar(lab_mask[:], lab_iota[:], lab_f, None, ALU.is_equal).then_inc(masks, 1)
            split_x_lo(3, 3)
            dve.wait_ge(hi_done, len(PIECES) + 1)
            lo = slice(2 * RANK, 3 * RANK)
            v.scalar_tensor_tensor(b_stack[lo, :], b_raw[lo, :], LORA_SCALING, f32(b_stack[lo, :]),
                                   ALU.mult, ALU.subtract).then_inc(b_split, 1)
            dve.wait_ge(masks, 1)

            def take_x1(h, y):
                dve.wait_ge(y_done, h + 1)
                v.memset(wait_mark[:, y:y + 1], 0.0)
                xh = x_all[:, bass.ds(h, 1), :].rearrange("p o (b n) -> p (o b) n", b=2)
                v.tensor_copy(xh, y1[y]).then_inc(y_read, 1)

            def select_low(h, p, y):
                dve.wait_ge(low_done, h + 1)
                v.tensor_tensor(low_prod[:, p, :], low_ps[y], lab_mask[:].rearrange("p l r -> p (l r)"),
                                ALU.mult).then_inc(low_read, 1)
                dve.wait_ge(low_read, h + 1)
                v.tensor_reduce(low_sel[:, p, :], low_prod[:, p, :].rearrange("p (l r) -> p r l", l=NLAB),
                                AX.X, ALU.add).then_inc(sel_done, 1)

            def split_low(h, p):
                dve.wait_ge(lowst_hi, h + 1)
                v.tensor_tensor(low_stack[RANK:2 * RANK, p, :], lowt_ps[0:RANK, p, 0:P],
                                f32(low_stack[0:RANK, p, :]), ALU.subtract).then_inc(lowst_done, 1)

            def pass1(h, p, last=False, last_y=None):
                take_x1(h - 1, 1 - p if last_y is None else last_y)
                select_low(h, p, p)
                split_low(h, p)
                if last:
                    split_x1_lo(h + 2 - H, p)
                else:
                    split_x_lo(h + 2, p)

            def heads(first, last):
                with dve.Fori(0, (last - first) // UNROLL) as turn:
                    for u in range(UNROLL):
                        pass1(turn * UNROLL + first + u, (first + u) % 2)

            y_of = (1, 0, 2)
            select_low(0, 0, y_of[0])
            select_low(1, 1, y_of[1])
            split_low(0, 0)
            select_low(2, 0, y_of[2])
            split_low(1, 1)
            take_x1(0, y_of[0])
            split_low(2, 0)
            take_x1(1, y_of[1])
            split_x_lo(4, 0)
            v.tensor_scalar(len_mask[:], l_iota[:], len_f, None, ALU.is_lt).then_inc(masks, 1)
            pass1(3, 1, last_y=y_of[2])
            heads(UNROLL, DVE_KGEN_HEAD)
            dve.wait_ge(k_den, 1)
            v.reciprocal(recip[:], tmp[:, 2, :]).then_inc(k_recip, 1)
            heads(DVE_KGEN_HEAD, T_HEAD)
            for h in range(T_HEAD, H):
                pass1(h, h % 2, last=h + 2 >= H)
            take_x1(H - 1, 1)

            def pass2(h, u, ahead=True):
                if ahead:
                    split_x1_lo(h + 1, (u + 1) % 2)
                dve.wait_ge(y_done, h + H + 1)
                v.memset(wait_mark[:, u:u + 1], 0.0)
                dve.wait_ge(masks, 2)
                v.copy_predicated(x_slot[:, u, :], len_mask[:], y2[u % 2][:, ::-1]).then_inc(y_read, 1)

            for h in range(FIRST):
                pass2(h, h, ahead=h > 0)
            with dve.Fori(0, TURNS) as turn:
                for u in range(TR):
                    pass2(turn * TR + FIRST + u, (FIRST + u) % TR)
            for h in range(LAST, H - 1):
                pass2(h, h % TR)
            u, p = (H - 1) % TR, (H - 1) % 2
            for half in range(2):
                cols = slice(half * HALF, (half + 1) * HALF)
                dve.wait_ge(y_done, 2 * H + half)
                v.copy_predicated(x_slot[:, u, cols], len_mask[:, cols],
                                  y_ps[p][:, half, 0:HALF][:, ::-1]).then_inc(y_read, 1)


def kernel(x, itok_B_0_2, itok_B_78_3631, L0_cond_W, L0_cond_lora_A, L0_cond_lora_B_w,
           L1_cond_log_dt, L1_cond_C, L1_cond_log_A_real, L1_cond_A_imag, L1_cond_D):
    import numpy as np
    import concourse.bacc as bacc
    from concourse.bass_utils import run_bass_kernel_spmd

    C = np.asarray(L1_cond_C)
    ssm = np.stack([np.asarray(L1_cond_log_A_real).T, np.asarray(L1_cond_A_imag).T,
                    C[:, :, 0].T, C[:, :, 1].T], axis=1)
    arrays = {
        "xt": np.asarray(x).reshape(P, H, CH, P).transpose(3, 1, 2, 0).reshape(P, H, L),
        "idx": np.stack([np.asarray(itok_B_0_2), np.asarray(itok_B_78_3631)], axis=1),
        "wa": np.concatenate([np.asarray(L0_cond_W).T,
                              np.asarray(L0_cond_lora_A).transpose(1, 0, 2).reshape(L, LOW)], axis=1),
        "lora_bt": np.asarray(L0_cond_lora_B_w).T,
        "log_dt": np.asarray(L1_cond_log_dt),
        "ssm": ssm,
        "d_skip": np.asarray(L1_cond_D),
    }
    arrays = {"in_" + k: np.ascontiguousarray(v) for k, v in arrays.items()}
    nc = bacc.Bacc("TRN2", target_bir_lowering=False, num_devices=1)
    args = [nc.dram_tensor(k, v.shape, mybir.dt.from_np(v.dtype), kind="ExternalInput").ap()
            for k, v in arrays.items()]
    out = nc.dram_tensor("out_0", (P, H, L), F32, kind="ExternalOutput").ap()
    conditioned_residual(nc, *args, out)
    r = run_bass_kernel_spmd(nc, [arrays], core_ids=[0])
    return r.results[0]["out_0"]
```
